# Optimizing a Trainium2 kernel written in Bass

```python
import numpy as np
import jax
import jax.numpy as jnp

def _softmax(x, axis=-1):
    return jax.nn.softmax(x, axis=axis)

def _gelu(x):
    return jax.nn.gelu(x, approximate=True)

def _silu(x):
    return jax.nn.silu(x)

def _sigmoid(x):
    return jax.nn.sigmoid(x)

def _layernorm(x, axis=-1, eps=1e-05):
    m = jnp.mean(x, axis=axis, keepdims=True)
    v = jnp.var(x, axis=axis, keepdims=True)
    return (x - m) / jnp.sqrt(v + eps)

def _scatter_add(tgt, idx, src, axis=0):
    return tgt.at[idx].add(src)

def _segment_sum(src, seg, n):
    return jax.ops.segment_sum(src, seg, n)
kernel_name = 'mk_hybrid_d1_jaxref_r4_06913e'

def setup_inputs(seed: int=0):
    np.random.seed(seed)
    _w = jnp.asarray

    def _L0_attn_a_setup():
        import jax, jax.numpy as jnp
        import numpy as np
        N_LAYERS = 2
        D_MODEL = 256
        D_INNER = 2 * D_MODEL
        D_STATE = 16
        D_CONV = 4
        DT_RANK = D_MODEL // 16
        B_SZ, L = (1, 512)
        EPS = 1e-05

        def layernorm(x, w, b):
            mu = jnp.mean(x, axis=-1, keepdims=True)
            var = jnp.mean(jnp.square(x - mu), axis=-1, keepdims=True)
            return (x - mu) * jax.lax.rsqrt(var + EPS) * w + b

        def mamba(x, in_w, cw, cb, xp_w, dtp_w, dtp_b, A_log, Dp, out_w):
            Bn, Ln, _ = x.shape
            xz = jnp.einsum('bld,ed->ble', x, in_w)
            xc, z = jnp.split(xz, 2, axis=-1)
            xp = jnp.pad(xc, ((0, 0), (D_CONV - 1, 0), (0, 0)))
            xc = sum((xp[:, k:k + Ln, :] * cw[:, k] for k in range(D_CONV))) + cb
            xc = jax.nn.silu(xc)
            dbl = jnp.einsum('ble,re->blr', xc, xp_w)
            dt, Bm, Cm = jnp.split(dbl, [DT_RANK, DT_RANK + D_STATE], axis=-1)
            dt = jax.nn.softplus(jnp.einsum('blr,er->ble', dt, dtp_w) + dtp_b)
            A = -jnp.exp(A_log)
            dA = jnp.exp(dt[..., None] * A)
            dBu = (dt * xc)[..., None] * Bm[:, :, None, :]

            def step(h, inp):
                dA_t, dBu_t, C_t = inp
                h = dA_t * h + dBu_t
                y = jnp.einsum('ben,bn->be', h, C_t)
                return (h, y)
            h0 = jnp.zeros((Bn, D_INNER, D_STATE), dA.dtype)
            _, ys = jax.lax.scan(step, h0, (dA.transpose(1, 0, 2, 3), dBu.transpose(1, 0, 2, 3), Cm.transpose(1, 0, 2)))
            y = ys.transpose(1, 0, 2) + xc * Dp
            y = y * jax.nn.silu(z)
            return jnp.einsum('ble,de->bld', y, out_w)
        key = jax.random.key(seed)
        ks = jax.random.split(key, 12)
        s = 0.02
        dt_init = np.log(np.expm1(0.01)).astype(np.float32)
        A_row = jnp.log(jnp.arange(1, D_STATE + 1, dtype=jnp.float32))
        return {'x': jax.random.normal(ks[0], (B_SZ, L, D_MODEL), jnp.float32), 'ln_w': jnp.ones((N_LAYERS, D_MODEL), jnp.float32), 'ln_b': jnp.zeros((N_LAYERS, D_MODEL), jnp.float32), 'in_proj_w': jax.random.normal(ks[1], (N_LAYERS, 2 * D_INNER, D_MODEL)) * s, 'conv_w': jax.random.normal(ks[2], (N_LAYERS, D_INNER, D_CONV)) * 0.2, 'conv_b': jnp.zeros((N_LAYERS, D_INNER), jnp.float32), 'x_proj_w': jax.random.normal(ks[3], (N_LAYERS, DT_RANK + 2 * D_STATE, D_INNER)) * s, 'dt_proj_w': jax.random.normal(ks[4], (N_LAYERS, D_INNER, DT_RANK)) * DT_RANK ** (-0.5), 'dt_proj_b': jnp.full((N_LAYERS, D_INNER), dt_init), 'A_log': jnp.broadcast_to(A_row, (N_LAYERS, D_INNER, D_STATE)).copy(), 'D_skip': jnp.ones((N_LAYERS, D_INNER), jnp.float32), 'out_proj_w': jax.random.normal(ks[5], (N_LAYERS, D_MODEL, D_INNER)) * s, 'norm_f_w': jnp.ones((D_MODEL,), jnp.float32), 'norm_f_b': jnp.zeros((D_MODEL,), jnp.float32)}
    _L0_attn_a_in = _L0_attn_a_setup()

    def _L0_attn_b_setup():
        import jax, jax.numpy as jnp
        import numpy as np
        D_MODEL = 256
        N_HEADS = 16
        HEAD_DIM = D_MODEL // N_HEADS
        WINDOW = 64
        key = jax.random.key(seed)
        ks = jax.random.split(key, 5)
        s = 1.0 / np.sqrt(D_MODEL)
        x = jax.random.normal(ks[0], (1, 1024, D_MODEL), dtype=jnp.float32)
        W_qkv = jax.random.uniform(ks[1], (D_MODEL, 3 * D_MODEL), jnp.float32, -s, s)
        b_qkv = jax.random.uniform(ks[2], (3 * D_MODEL,), jnp.float32, -s, s)
        W_proj = jax.random.uniform(ks[3], (D_MODEL, D_MODEL), jnp.float32, -s, s)
        b_proj = jax.random.uniform(ks[4], (D_MODEL,), jnp.float32, -s, s)
        return {'x': x, 'W_qkv': W_qkv, 'b_qkv': b_qkv, 'W_proj': W_proj, 'b_proj': b_proj}
    _L0_attn_b_in = _L0_attn_b_setup()

    def _L0_ffn_setup():
        import jax, jax.numpy as jnp
        import numpy as np
        D_MODEL = 256
        NUM_SLOTS = 64
        TOP_K = 8
        B, T = (4, 1024)

        def _forward(x, slot_init, slot_scale, w1, b1, w2, b2, gru_wih, gru_whh, gru_bih, gru_bhh, wv, bv, wo, bo, tau):
            Bn, Tn, D = x.shape
            Sn = slot_init.shape[0]
            S = jnp.broadcast_to((slot_init * slot_scale)[None], (Bn, Sn, D)).astype(x.dtype)
            slot_mean = S.mean(axis=1, keepdims=True)
            ctx = jnp.concatenate([x, jnp.broadcast_to(slot_mean, x.shape)], axis=-1)
            h = jax.nn.gelu(ctx @ w1.T + b1, approximate=False)
            route_logits = (h @ w2.T + b2) / (jnp.abs(tau) + 0.1)
            topk_vals, topk_idx = jax.lax.top_k(route_logits, TOP_K)
            topk_w = jax.nn.softmax(topk_vals, axis=-1)
            alpha = jnp.sum(topk_w[..., None] * jax.nn.one_hot(topk_idx, Sn, dtype=x.dtype), axis=-2)
            slot_input = jnp.einsum('bts,btd->bsd', alpha, x)
            slot_wsum = alpha.sum(axis=1) + 1e-08
            gi = (slot_input / slot_wsum[..., None]).reshape(Bn * Sn, D)
            hs = S.reshape(Bn * Sn, D)
            gx = gi @ gru_wih.T + gru_bih
            gh = hs @ gru_whh.T + gru_bhh
            xr, xz, xn = jnp.split(gx, 3, axis=-1)
            hr, hz, hn = jnp.split(gh, 3, axis=-1)
            r = jax.nn.sigmoid(xr + hr)
            z = jax.nn.sigmoid(xz + hz)
            n = jnp.tanh(xn + r * hn)
            h_new = (1.0 - z) * n + z * hs
            S_new = h_new.reshape(Bn, Sn, D)
            slot_values = S_new @ wv.T + bv
            out = jnp.einsum('bts,bsd->btd', alpha, slot_values)
            return out @ wo.T + bo
        key = jax.random.key(seed)
        ks = jax.random.split(key, 16)
        D, S = (D_MODEL, NUM_SLOTS)
        H = D // 2
        sc = lambda fan_in: 1.0 / np.sqrt(fan_in)
        inp = {'x': jax.random.normal(ks[0], (B, T, D), dtype=jnp.float32), 'slot_init': jax.random.normal(ks[1], (S, D), dtype=jnp.float32) * 0.1, 'slot_scale': jnp.ones((S, 1), dtype=jnp.float32), 'w1': jax.random.normal(ks[2], (H, 2 * D), dtype=jnp.float32) * sc(2 * D), 'b1': jnp.zeros((H,), dtype=jnp.float32), 'w2': jax.random.normal(ks[3], (S, H), dtype=jnp.float32) * sc(H), 'b2': jnp.zeros((S,), dtype=jnp.float32), 'gru_wih': jax.random.normal(ks[4], (3 * D, D), dtype=jnp.float32) * sc(D), 'gru_whh': jax.random.normal(ks[5], (3 * D, D), dtype=jnp.float32) * sc(D), 'gru_bih': jnp.zeros((3 * D,), dtype=jnp.float32), 'gru_bhh': jnp.zeros((3 * D,), dtype=jnp.float32), 'wv': jax.random.normal(ks[6], (D, D), dtype=jnp.float32) * sc(D), 'bv': jnp.zeros((D,), dtype=jnp.float32), 'wo': jax.random.normal(ks[7], (D, D), dtype=jnp.float32) * sc(D), 'bo': jnp.zeros((D,), dtype=jnp.float32), 'tau': jnp.ones((1,), dtype=jnp.float32)}
        return inp
    _L0_ffn_in = _L0_ffn_setup()
    _d = {'L0_attn_a_x': _L0_attn_a_in['x'], 'L0_attn_a_ln_w': _L0_attn_a_in['ln_w'], 'L0_attn_a_ln_b': _L0_attn_a_in['ln_b'], 'L0_attn_a_in_proj_w': _L0_attn_a_in['in_proj_w'], 'L0_attn_a_conv_w': _L0_attn_a_in['conv_w'], 'L0_attn_a_conv_b': _L0_attn_a_in['conv_b'], 'L0_attn_a_x_proj_w': _L0_attn_a_in['x_proj_w'], 'L0_attn_a_dt_proj_w': _L0_attn_a_in['dt_proj_w'], 'L0_attn_a_dt_proj_b': _L0_attn_a_in['dt_proj_b'], 'L0_attn_a_A_log': _L0_attn_a_in['A_log'], 'L0_attn_a_D_skip': _L0_attn_a_in['D_skip'], 'L0_attn_a_out_proj_w': _L0_attn_a_in['out_proj_w'], 'L0_attn_a_norm_f_w': _L0_attn_a_in['norm_f_w'], 'L0_attn_a_norm_f_b': _L0_attn_a_in['norm_f_b'], 'L0_attn_b_W_qkv': _L0_attn_b_in['W_qkv'], 'L0_attn_b_b_qkv': _L0_attn_b_in['b_qkv'], 'L0_attn_b_W_proj': _L0_attn_b_in['W_proj'], 'L0_attn_b_b_proj': _L0_attn_b_in['b_proj'], 'L0_ffn_slot_init': _L0_ffn_in['slot_init'], 'L0_ffn_slot_scale': _L0_ffn_in['slot_scale'], 'L0_ffn_w1': _L0_ffn_in['w1'], 'L0_ffn_b1': _L0_ffn_in['b1'], 'L0_ffn_w2': _L0_ffn_in['w2'], 'L0_ffn_b2': _L0_ffn_in['b2'], 'L0_ffn_gru_wih': _L0_ffn_in['gru_wih'], 'L0_ffn_gru_whh': _L0_ffn_in['gru_whh'], 'L0_ffn_gru_bih': _L0_ffn_in['gru_bih'], 'L0_ffn_gru_bhh': _L0_ffn_in['gru_bhh'], 'L0_ffn_wv': _L0_ffn_in['wv'], 'L0_ffn_bv': _L0_ffn_in['bv'], 'L0_ffn_wo': _L0_ffn_in['wo'], 'L0_ffn_bo': _L0_ffn_in['bo'], 'L0_ffn_tau': _L0_ffn_in['tau']}
    _x0 = _d['L0_attn_a_x']
    _d['L0_attn_a_x'] = jax.random.normal(jax.random.fold_in(jax.random.key(seed), 1), (2, 2048, 256), dtype=_x0.dtype)
    del _x0
    return _d

def reference(L0_attn_a_x, L0_attn_a_ln_w, L0_attn_a_ln_b, L0_attn_a_in_proj_w, L0_attn_a_conv_w, L0_attn_a_conv_b, L0_attn_a_x_proj_w, L0_attn_a_dt_proj_w, L0_attn_a_dt_proj_b, L0_attn_a_A_log, L0_attn_a_D_skip, L0_attn_a_out_proj_w, L0_attn_a_norm_f_w, L0_attn_a_norm_f_b, L0_attn_b_W_qkv, L0_attn_b_b_qkv, L0_attn_b_W_proj, L0_attn_b_b_proj, L0_ffn_slot_init, L0_ffn_slot_scale, L0_ffn_w1, L0_ffn_b1, L0_ffn_w2, L0_ffn_b2, L0_ffn_gru_wih, L0_ffn_gru_whh, L0_ffn_gru_bih, L0_ffn_gru_bhh, L0_ffn_wv, L0_ffn_bv, L0_ffn_wo, L0_ffn_bo, L0_ffn_tau):

    def _L0_attn_a_ref(x, ln_w, ln_b, in_proj_w, conv_w, conv_b, x_proj_w, dt_proj_w, dt_proj_b, A_log, D_skip, out_proj_w, norm_f_w, norm_f_b):
        import jax, jax.numpy as jnp
        import numpy as np
        N_LAYERS = 2
        D_MODEL = 256
        D_INNER = 2 * D_MODEL
        D_STATE = 16
        D_CONV = 4
        DT_RANK = D_MODEL // 16
        B_SZ, L = (1, 512)
        EPS = 1e-05

        def layernorm(x, w, b):
            mu = jnp.mean(x, axis=-1, keepdims=True)
            var = jnp.mean(jnp.square(x - mu), axis=-1, keepdims=True)
            return (x - mu) * jax.lax.rsqrt(var + EPS) * w + b

        def mamba(x, in_w, cw, cb, xp_w, dtp_w, dtp_b, A_log, Dp, out_w):
            Bn, Ln, _ = x.shape
            xz = jnp.einsum('bld,ed->ble', x, in_w)
            xc, z = jnp.split(xz, 2, axis=-1)
            xp = jnp.pad(xc, ((0, 0), (D_CONV - 1, 0), (0, 0)))
            xc = sum((xp[:, k:k + Ln, :] * cw[:, k] for k in range(D_CONV))) + cb
            xc = jax.nn.silu(xc)
            dbl = jnp.einsum('ble,re->blr', xc, xp_w)
            dt, Bm, Cm = jnp.split(dbl, [DT_RANK, DT_RANK + D_STATE], axis=-1)
            dt = jax.nn.softplus(jnp.einsum('blr,er->ble', dt, dtp_w) + dtp_b)
            A = -jnp.exp(A_log)
            dA = jnp.exp(dt[..., None] * A)
            dBu = (dt * xc)[..., None] * Bm[:, :, None, :]

            def step(h, inp):
                dA_t, dBu_t, C_t = inp
                h = dA_t * h + dBu_t
                y = jnp.einsum('ben,bn->be', h, C_t)
                return (h, y)
            h0 = jnp.zeros((Bn, D_INNER, D_STATE), dA.dtype)
            _, ys = jax.lax.scan(step, h0, (dA.transpose(1, 0, 2, 3), dBu.transpose(1, 0, 2, 3), Cm.transpose(1, 0, 2)))
            y = ys.transpose(1, 0, 2) + xc * Dp
            y = y * jax.nn.silu(z)
            return jnp.einsum('ble,de->bld', y, out_w)
        for i in range(N_LAYERS):
            h = layernorm(x, ln_w[i], ln_b[i])
            h = mamba(h, in_proj_w[i], conv_w[i], conv_b[i], x_proj_w[i], dt_proj_w[i], dt_proj_b[i], A_log[i], D_skip[i], out_proj_w[i])
            x = h + x
        return layernorm(x, norm_f_w, norm_f_b)

    def _L0_attn_b_ref(x, W_qkv, b_qkv, W_proj, b_proj):
        import jax, jax.numpy as jnp
        import numpy as np
        D_MODEL = 256
        N_HEADS = 16
        HEAD_DIM = D_MODEL // N_HEADS
        WINDOW = 64
        b, t, c = x.shape
        qkv = x @ W_qkv + b_qkv
        q, k, v = jnp.split(qkv, 3, axis=-1)
        q = q.reshape(b, t, N_HEADS, HEAD_DIM).transpose(0, 2, 1, 3)
        k = k.reshape(b, t, N_HEADS, HEAD_DIM).transpose(0, 2, 1, 3)
        v = v.reshape(b, t, N_HEADS, HEAD_DIM).transpose(0, 2, 1, 3)
        att = jnp.einsum('bhqd,bhkd->bhqk', q, k) / np.sqrt(HEAD_DIM)
        idx = jnp.arange(t)
        diff = idx[:, None] - idx[None, :]
        allowed = (diff >= 0) & (diff < WINDOW)
        att = jnp.where(allowed[None, None], att, -jnp.inf)
        att = jax.nn.softmax(att, axis=-1)
        y = jnp.einsum('bhqk,bhkd->bhqd', att, v)
        y = y.transpose(0, 2, 1, 3).reshape(b, t, c)
        return y @ W_proj + b_proj

    def _L0_ffn_ref(x, slot_init, slot_scale, w1, b1, w2, b2, gru_wih, gru_whh, gru_bih, gru_bhh, wv, bv, wo, bo, tau):
        import jax, jax.numpy as jnp
        import numpy as np
        D_MODEL = 256
        NUM_SLOTS = 64
        TOP_K = 8
        B, T = (4, 1024)

        def _forward(x, slot_init, slot_scale, w1, b1, w2, b2, gru_wih, gru_whh, gru_bih, gru_bhh, wv, bv, wo, bo, tau):
            Bn, Tn, D = x.shape
            Sn = slot_init.shape[0]
            S = jnp.broadcast_to((slot_init * slot_scale)[None], (Bn, Sn, D)).astype(x.dtype)
            slot_mean = S.mean(axis=1, keepdims=True)
            ctx = jnp.concatenate([x, jnp.broadcast_to(slot_mean, x.shape)], axis=-1)
            h = jax.nn.gelu(ctx @ w1.T + b1, approximate=False)
            route_logits = (h @ w2.T + b2) / (jnp.abs(tau) + 0.1)
            topk_vals, topk_idx = jax.lax.top_k(route_logits, TOP_K)
            topk_w = jax.nn.softmax(topk_vals, axis=-1)
            alpha = jnp.sum(topk_w[..., None] * jax.nn.one_hot(topk_idx, Sn, dtype=x.dtype), axis=-2)
            slot_input = jnp.einsum('bts,btd->bsd', alpha, x)
            slot_wsum = alpha.sum(axis=1) + 1e-08
            gi = (slot_input / slot_wsum[..., None]).reshape(Bn * Sn, D)
            hs = S.reshape(Bn * Sn, D)
            gx = gi @ gru_wih.T + gru_bih
            gh = hs @ gru_whh.T + gru_bhh
            xr, xz, xn = jnp.split(gx, 3, axis=-1)
            hr, hz, hn = jnp.split(gh, 3, axis=-1)
            r = jax.nn.sigmoid(xr + hr)
            z = jax.nn.sigmoid(xz + hz)
            n = jnp.tanh(xn + r * hn)
            h_new = (1.0 - z) * n + z * hs
            S_new = h_new.reshape(Bn, Sn, D)
            slot_values = S_new @ wv.T + bv
            out = jnp.einsum('bts,bsd->btd', alpha, slot_values)
            return out @ wo.T + bo
        return _forward(x, slot_init, slot_scale, w1, b1, w2, b2, gru_wih, gru_whh, gru_bih, gru_bhh, wv, bv, wo, bo, tau)
    x = L0_attn_a_x
    x = x + _L0_attn_a_ref(_layernorm(x, axis=-1), L0_attn_a_ln_w, L0_attn_a_ln_b, L0_attn_a_in_proj_w, L0_attn_a_conv_w, L0_attn_a_conv_b, L0_attn_a_x_proj_w, L0_attn_a_dt_proj_w, L0_attn_a_dt_proj_b, L0_attn_a_A_log, L0_attn_a_D_skip, L0_attn_a_out_proj_w, L0_attn_a_norm_f_w, L0_attn_a_norm_f_b)
    x = x + _L0_ffn_ref(_layernorm(x, axis=-1), L0_ffn_slot_init, L0_ffn_slot_scale, L0_ffn_w1, L0_ffn_b1, L0_ffn_w2, L0_ffn_b2, L0_ffn_gru_wih, L0_ffn_gru_whh, L0_ffn_gru_bih, L0_ffn_gru_bhh, L0_ffn_wv, L0_ffn_bv, L0_ffn_wo, L0_ffn_bo, L0_ffn_tau)
    x = x + _L0_attn_b_ref(_layernorm(x, axis=-1), L0_attn_b_W_qkv, L0_attn_b_b_qkv, L0_attn_b_W_proj, L0_attn_b_b_proj)
    x = x + _L0_ffn_ref(_layernorm(x, axis=-1), L0_ffn_slot_init, L0_ffn_slot_scale, L0_ffn_w1, L0_ffn_b1, L0_ffn_w2, L0_ffn_b2, L0_ffn_gru_wih, L0_ffn_gru_whh, L0_ffn_gru_bih, L0_ffn_gru_bhh, L0_ffn_wv, L0_ffn_bv, L0_ffn_wo, L0_ffn_bo, L0_ffn_tau)
    return x

_drawn_inputs = setup_inputs


def setup_inputs(seed=0):
    import zlib

    import numpy as np

    out = dict(_drawn_inputs(seed))
    spreads = {'L0_attn_a_ln_w': (1.0, 0.6),
     'L0_attn_a_ln_b': (0.0, 0.8),
     'L0_attn_a_conv_b': (0.0, 0.8),
     'L0_attn_a_dt_proj_b': (-4.600165843963623, 0.6),
     'L0_attn_a_D_skip': (1.0, 0.6),
     'L0_attn_a_norm_f_w': (1.0, 0.2),
     'L0_attn_a_norm_f_b': (0.0, 0.1),
     'L0_ffn_slot_scale': (1.0, 0.6),
     'L0_ffn_b1': (0.0, 0.788),
     'L0_ffn_b2': (0.0, 0.63),
     'L0_ffn_gru_bih': (0.0, 0.1),
     'L0_ffn_gru_bhh': (0.0, 0.384),
     'L0_ffn_bv': (0.0, 0.1),
     'L0_ffn_bo': (0.0, 0.1)}
    factors = {'L0_attn_a_in_proj_w': 8.0,
     'L0_attn_a_conv_w': 8.0,
     'L0_attn_a_x_proj_w': 8.0,
     'L0_attn_a_dt_proj_w': 8.0,
     'L0_attn_a_A_log': 8.0,
     'L0_attn_a_out_proj_w': 8.0,
     'L0_attn_b_b_qkv': 4.688,
     'L0_attn_b_b_proj': 3.266,
     'L0_ffn_slot_init': 2.747,
     'L0_ffn_gru_whh': 6.232}
    for name, (base, spread) in spreads.items():
        noise = np.random.default_rng([zlib.crc32(name.encode()), seed]).standard_normal(out[name].shape)
        drawn = base * np.exp(spread * noise) if base else spread * noise
        out[name] = jnp.asarray(drawn.astype(out[name].dtype))
    for name, factor in factors.items():
        out[name] = (out[name] * factor).astype(out[name].dtype)
    return out
```

```python
from contextlib import ExitStack

import concourse.bass as bass
from concourse import mybir

F32 = mybir.dt.float32
BF16 = mybir.dt.bfloat16
ALU = mybir.AluOpType
ACT = mybir.ActivationFunctionType
AX = mybir.AxisListType.X

P = 128
D = 256
KT = D // P
TOK = 4096
EPS = 1e-5
SERIES = 1.0 / 32
NEG = -1.0e30

LAYERS = 2
DI = 512
CT = DI // P
NS = 16
R = 16
DC = 4
T = 1024
TT = T // P
CHUNKS = 2
BATCH = 2
HALF = 512
EU = P // NS
GC = 32
JU = GC // EU
QU = P // GC
UNITS = CT * JU * QU
TU = JU * QU
PARTS = 3

C_IN = 0
C_OUT = C_IN + KT * 2 * DI
C_XP = C_OUT + CT * D
C_A = C_XP + CT * (R + 2 * NS)
C_CW = C_A + UNITS
C_CB = C_CW + CT * DC
C_DTB = C_CB + CT
C_DS = C_DTB + CT
C_LNW = C_DS + CT
C_LNB = C_LNW + KT
C_ALL = C_LNB + KT


class Signals:

    def __init__(self, nc):
        self.nc, self.held = nc, []

    def add(self, name):
        self.held.append(self.nc.alloc_semaphore(name))
        return self.held[-1]

    def clear(self):
        self.nc.all_engine_barrier()
        self.nc.clear_and_free_semaphores(self.held)
        self.nc.all_engine_barrier()


class Chain:

    def __init__(self, eng, sem, base=0):
        self.eng, self.sem, self.base, self.n = eng, sem, base, 0

    def add(self, ins):
        ins.then_inc(self.sem, 1)
        self.n += 1
        return self.n

    def wait(self, n=None):
        self.eng.wait_ge(self.sem, self.base + (self.n if n is None else n))

    def link(self, ins):
        self.add(ins)
        self.wait()


def first_norm(nc, x, r0):
    TG = 8
    NG = TOK // P // TG
    xv = x.rearrange("(g i p) d -> g p i d", i=TG, p=P)
    rv = r0.rearrange("(g i p) d -> g p i d", i=TG, p=P)
    with ExitStack() as ctx:
        sb = lambda n, s, d=F32: ctx.enter_context(nc.sbuf_tensor(n, s, d))
        signals = Signals(nc)
        sem = signals.add
        xt = sb("n0_x", [P, NG, TG, D])
        st = sb("n0_stats", [P, TG, 6])
        mv = sb("n0_meanvar", [P, NG, TG, 2])
        ve = sb("n0_vareps", [P, NG, TG])
        half = sb("n0_minushalf", [P, TG])
        rs = sb("n0_rstd", [P, NG, TG])
        s_half = sem("n0_half_set")
        s_ld = [sem(f"n0_loaded{g}") for g in range(NG)]
        s_v = sem("n0_vector")
        s_ve = sem("n0_var_ready")
        s_rs = sem("n0_rstd_ready")
        s_n = sem("n0_normed")
        s_st = sem("n0_stored")
        with nc.Block() as block:
            @block.sync
            def _(sp):
                for g in range(NG):
                    sp.dma_start(xt[:, g], xv[g]).then_inc(s_ld[g], 16)
                for g in range(NG):
                    sp.wait_ge(s_n, g + 1)
                    sp.dma_start(rv[g], xt[:, g]).then_inc(s_st, 16)
                sp.wait_ge(s_st, 16 * NG)

            @block.vector
            def _(dve):
                own = Chain(dve, s_v)
                for g in range(NG):
                    dve.wait_ge(s_ld[g], 16)
                    first = own.n
                    for i in range(TG):
                        own.add(dve.bn_stats(st[:, i], xt[:, g, i]))
                    for i in range(TG):
                        own.wait(first + i + 1)
                        own.add(dve.bn_aggr(mv[:, g, i], st[:, i]))
                    own.wait()
                    own.add(dve.tensor_scalar(ve[:, g], mv[:, g, :, 1], EPS, None, ALU.add))
                    own.wait()
                    dve.sem_inc(s_ve, 1)
                    dve.wait_ge(s_rs, g + 1)
                    for i in range(TG):
                        own.add(dve.tensor_scalar(xt[:, g, i], xt[:, g, i], mv[:, g, i, 0:1], rs[:, g, i:i + 1],
                                                  ALU.subtract, ALU.mult))
                    own.wait()
                    dve.sem_inc(s_n, 1)

            @block.gpsimd
            def _(pool):
                pool.memset(half[:], -0.5).then_inc(s_half, 1)
                pool.wait_ge(s_half, 1)
                for g in range(NG):
                    pool.wait_ge(s_ve, g + 1)
                    pool.tensor_tensor(rs[:, g], ve[:, g], half[:], ALU.pow).then_inc(s_rs, 1)
        signals.clear()


def second_norm(nc, x, r, out, norm_in):
    TG = 8
    NG = TOK // P // TG
    xv = x.rearrange("(g i p) d -> g p i d", i=TG, p=P)
    rv = r.rearrange("(g i p) d -> g p i d", i=TG, p=P)
    ov = out.rearrange("(g i p) d -> g p i d", i=TG, p=P)
    with ExitStack() as ctx:
        sb = lambda n, s, d=F32: ctx.enter_context(nc.sbuf_tensor("n1_" + n, s, d))
        signals = Signals(nc)
        sem = lambda n: signals.add("n1_" + n)
        wb = sb("w_b", [P, 2, D])
        xt = sb("x", [P, NG, TG, D])
        rt = sb("r", [P, NG, TG, D])
        st = sb("stats", [P, TG, 6])
        mv = sb("meanvar", [P, NG, TG, 2])
        ve = sb("vareps", [P, NG, TG])
        half = sb("minushalf", [P, TG])
        rs = sb("rstd", [P, NG, TG])
        s_half, s_w, s_v, s_ve, s_rs, s_xb, s_n, s_out, s_st = (
            sem(n) for n in "half_set w_loaded vector var_ready rstd_ready x_bias_ready normed out_ready stored".split())
        s_ld = [sem(f"loaded{g}") for g in range(NG)]
        with nc.Block() as block:
            @block.sync
            def _(sp):
                sp.dma_start(wb[:], norm_in).then_inc(s_w, 16)
                for g in range(NG):
                    sp.dma_start(rt[:, g], rv[g]).then_inc(s_ld[g], 16)
                    sp.dma_start(xt[:, g], xv[g]).then_inc(s_ld[g], 16)
                for g in range(NG):
                    sp.wait_ge(s_out, g + 1)
                    sp.dma_start(ov[g], rt[:, g]).then_inc(s_st, 16)
                sp.wait_ge(s_st, 16 * NG)

            @block.vector
            def _(dve):
                own = Chain(dve, s_v)
                dve.wait_ge(s_w, 16)
                for g in range(NG):
                    first = own.n
                    dve.wait_ge(s_ld[g], 32)
                    for i in range(TG):
                        own.add(dve.bn_stats(st[:, i], rt[:, g, i]))
                    for i in range(TG):
                        own.wait(first + i + 1)
                        own.add(dve.bn_aggr(mv[:, g, i], st[:, i]))
                    own.wait()
                    dve.tensor_scalar(ve[:, g], mv[:, g, :, 1], EPS, None, ALU.add).then_inc(s_ve, 1)
                    dve.wait_ge(s_rs, g + 1)
                    for i in range(TG):
                        own.add(dve.tensor_scalar(rt[:, g, i], rt[:, g, i], mv[:, g, i, 0:1], rs[:, g, i:i + 1],
                                                  ALU.subtract, ALU.mult))
                    own.wait()
                    dve.tensor_tensor(rt[:, g], rt[:, g], wb[:, 0:1].to_broadcast([P, TG, D]), ALU.mult)\
                        .then_inc(s_n, 1)
                    dve.wait_ge(s_n, g + 1)
                    dve.wait_ge(s_xb, g + 1)
                    dve.tensor_tensor(rt[:, g], rt[:, g], xt[:, g], ALU.add).then_inc(s_out, 1)

            @block.gpsimd
            def _(pool):
                pool.memset(half[:], -0.5).then_inc(s_half, 1)
                pool.wait_ge(s_half, 1)
                pool.wait_ge(s_w, 16)
                for g in range(NG):
                    pool.wait_ge(s_ve, g + 1)
                    pool.tensor_tensor(rs[:, g], ve[:, g], half[:], ALU.pow).then_inc(s_rs, 1)
                    pool.wait_ge(s_ld[g], 32)
                    pool.tensor_tensor(xt[:, g], xt[:, g], wb[:, 1:2].to_broadcast([P, TG, D]), ALU.add)\
                        .then_inc(s_xb, 1)
        signals.clear()


def mamba(nc, r, packs, dtw_in, consts):
    ident_in, selj_in, sely_in, selbc_in = consts
    rv = r.rearrange("(s i p) d -> s p i d", i=TT, p=P)
    stack = nc.dram_tensor("dt_u_stack", [CT, 2, PARTS * GC, QU, T], BF16, kind="Internal").ap()
    with ExitStack() as ctx:
        sb = lambda n, s, d=F32: ctx.enter_context(nc.sbuf_tensor(n, s, d))
        signals = Signals(nc)
        sem = signals.add
        W = sb("weights", [P, C_ALL])
        DTW = sb("dt_weights", [R, DI])
        ident = sb("ident", [P, P])
        selj = sb("unit_select", [PARTS * GC, JU, P], BF16)
        sely = sb("state_sum", [P, JU, GC])
        selbc = sb("bc_select", [R + 2 * NS, 2, P])
        A = sb("A", [P, UNITS])
        xt = sb("x_tok", [P, CHUNKS, TT, D])
        st = sb("ln_stats", [P, TT, 6])
        mv = sb("ln_meanvar", [P, TT, 2])
        ve = sb("ln_vareps", [P, TT])
        half = sb("minushalf", [P, TT])
        rs = sb("ln_rstd", [P, TT])
        hT = sb("h_feat", [P, KT, T])
        dbl = sb("dt_B_C", [R + 2 * NS, T])
        xp = sb("conv_in", [P, CT, DC - 1 + T])
        halo = sb("conv_halo", [P, CHUNKS + 1, CT, DC - 1])
        xc = sb("conv_out", [P, CT, T])
        sz = sb("silu_z", [P, CT, T])
        brep = sb("B_rep", [P, T])
        crep = sb("C_rep", [P, T])
        stk = sb("stacks", [PARTS * GC, 2, 2, QU, T], BF16)
        small = [sb(f"small_e{k}", [P, T], mybir.dt.uint8) for k in range(2)]
        carry = sb("h_carry", [P, CHUNKS + 1, UNITS])
        H, DB, HC = 4, 4, 8
        ring = sb("ring", [P, H + DB + HC, T])
        h = ring[:, 0:H]
        dbu = ring[:, H:H + DB]
        hc = ring[:, H + DB:]
        xh = ring[:, 0:2].rearrange("p a t -> p (a t)").rearrange("p (i d) -> p i d", d=D)
        tmp = [ring[:, 7 * k:7 * k + 4] for k in range(2)]
        prt = [ring[:, 7 * k + 4:7 * k + 7].bitcast(BF16).rearrange("p a (b t) -> p (a b) t", t=T) for k in range(2)]
        PS = ctx.enter_context(nc.psum_tensor("psum", [P, 8, HALF], F32))
        flat = lambda a, n: PS[:, a:a + n].rearrange("p a t -> p (a t)")

        names = ("const w_ld x_ld st_ld r_st half A_exp A_rdy zero gated stats dve dve_on pool_on pe_on sp_on ve rs xh tp hT "
                 "x_mm z_mm xp sz conv xc dbl_mm dbl bc_mm bc dt_mm abs relu exp ln ser0 ser1 ser2 ser3 small log1p dt dt_hi dt_r "
                 "dt_mid dt_parts u u_hi u_r u_mid u_parts dt_rep u_rep decay dbu scan kept hc ysum ygate o_mm res").split()
        S = {n: sem("m_" + n) for n in names}
        st_wr = [sem(f"m_stacks_written{ct}") for ct in range(CT)]
        WR = 2 * QU * 16
        STEPS = BATCH * CHUNKS

        with nc.Block() as block:
            @block.sync
            def _(sp):
                sp.dma_start(xt[:, 0], rv[0]).then_inc(S["x_ld"], 16)
                sp.dma_start(ident[:], ident_in).then_inc(S["const"], 16)
                sp.dma_start(selj[:], selj_in).then_inc(S["const"], 16)
                sp.dma_start(sely[:], sely_in).then_inc(S["const"], 16)
                sp.dma_start(selbc[:], selbc_in).then_inc(S["const"], 16)
                with sp.Fori(0, LAYERS) as l:
                    sp.wait_ge(S["res"], l * STEPS * TT)
                    sp.sem_inc(S["sp_on"], 1)
                    sp.wait_ge(S["ygate"], l * STEPS * CT)
                    sp.dma_start(W[:], packs[l]).then_inc(S["w_ld"], 16)
                    sp.dma_start(DTW[:], dtw_in[l]).then_inc(S["w_ld"], 16)
                    with sp.Fori(0, BATCH) as b:
                        with sp.Fori(0, CHUNKS) as c:
                            bc_ = b * CHUNKS + c
                            s = l * STEPS + bc_
                            sp.wait_ge(S["r_st"], s * 16)
                            sp.wait_ge(S["x_ld"], (s + 1) * 16)
                            sp.dma_start(xt[:, (c + 1) % CHUNKS], rv[(bc_ + 1) % STEPS]).then_inc(S["x_ld"], 16)
                            for ct in range(CT):
                                for te, name in ((0, "dt_parts"), (1, "u_parts")):
                                    if ct == 0 and te == 0:
                                        sp.wait_ge(S["st_ld"], s * CT * 32)
                                        sp.sem_inc(S["sp_on"], 1)
                                        sp.wait_ge(S["u_rep"], s * UNITS)
                                        sp.sem_inc(S["sp_on"], 1)
                                    sp.wait_ge(S[name], s * CT + ct + 1)
                                    for q in range(QU):
                                        src = prt[ct % 2][GC * q:GC * q + GC, PARTS * te:PARTS * te + PARTS]
                                        dst = stack[ct, te, :, q].rearrange("(a c) t -> c a t", c=GC)
                                        sp.dma_start(dst, src).then_inc(st_wr[ct], 16)
                                if ct == 1:
                                    sp.wait_ge(st_wr[0], (s + 1) * WR)
                                    for te2 in range(2):
                                        sp.dma_start(stk[:, 0, te2], stack[0, te2]).then_inc(S["st_ld"], 16)
                            for ct in range(1, CT):
                                sp.wait_ge(st_wr[ct], (s + 1) * WR)
                            sp.sem_inc(S["sp_on"], 1)
                            with sp.Fori(1, CT) as ct:
                                sp.wait_ge(S["u_rep"], (s * CT + ct - 1) * TU + 1)
                                for te in range(2):
                                    sp.dma_start(stk[:, ct % 2, te], stack[ct, te]).then_inc(S["st_ld"], 16)
                            sp.wait_ge(S["res"], (s + 1) * TT)
                            sp.dma_start(rv[bc_], xt[:, c]).then_inc(S["r_st"], 16)
                sp.wait_ge(S["r_st"], LAYERS * STEPS * 16)

            @block.vector
            def _(dve):
                for a in (halo, carry):
                    dve.memset(a[:], 0.0).then_inc(S["zero"], 1)

                def stats(s, buf):
                    own = Chain(dve, S["stats"], s * 2 * TT)
                    dve.wait_ge(S["x_ld"], (s + 1) * 16)
                    dve.sem_inc(S["dve_on"], 1)
                    for i in range(TT):
                        own.add(dve.bn_stats(st[:, i], xt[:, buf, i]))
                    own.wait()
                    dve.sem_inc(S["dve_on"], 1)
                    for i in range(TT):
                        own.add(dve.bn_aggr(mv[:, i], st[:, i]))
                    own.wait()
                    dve.tensor_scalar(ve[:], mv[:, :, 1], EPS, None, ALU.add).then_inc(S["ve"], 1)

                def normalise(s, buf):
                    dve.wait_ge(S["rs"], s + 1)
                    dve.wait_ge(S["kept"], s * UNITS)
                    dve.wait_ge(S["hc"], s * UNITS)
                    for i in range(TT):
                        dve.tensor_scalar(xh[:, i], xt[:, buf, i], mv[:, i, 0:1], rs[:, i:i + 1],
                                          ALU.subtract, ALU.mult).then_inc(S["xh"], 1)

                stats(0, 0)
                normalise(0, 0)
                with dve.Fori(0, LAYERS) as l:
                    dve.wait_ge(S["A_exp"], l + 1)
                    dve.tensor_scalar(A[:], A[:], -1.0, None, ALU.mult).then_inc(S["A_rdy"], 1)
                    with dve.Fori(0, BATCH) as b:
                        with dve.Fori(0, CHUNKS) as c:
                            s = (l * BATCH + b) * CHUNKS + c
                            PRE = 2 + CT * (DC - 1)
                            own = Chain(dve, S["dve"], s * PRE)
                            own.add(dve.tensor_copy(xp[:, :, 0:DC - 1], halo[:, c]))
                            for m in range(CT):
                                dve.wait_ge(S["xp"], s * CT + m + 1)
                                if m == 0:
                                    own.wait()
                                for k in range(DC):
                                    w = W[:, C_CW + m * DC + k:C_CW + m * DC + k + 1]
                                    if k == 0:
                                        ins = dve.tensor_scalar(xc[:, m], xp[:, m, 0:T], w,
                                                                W[:, C_CB + m:C_CB + m + 1], ALU.mult, ALU.add)
                                    else:
                                        ins = dve.scalar_tensor_tensor(xc[:, m], xp[:, m, k:k + T], w, xc[:, m],
                                                                       ALU.mult, ALU.add)
                                    if k < DC - 1:
                                        own.add(ins)
                                        own.wait()
                                    else:
                                        ins.then_inc(S["conv"], 1)
                            own.add(dve.tensor_copy(halo[:, 1], xp[:, :, T:]))
                            assert own.n == PRE
                            for pair in range(0, CT, 2):
                                two = [(ct, s * CT + ct + 1, *(tmp[ct % 2][:, i] for i in range(4)), prt[ct % 2])
                                       for ct in (pair, pair + 1)]
                                for ct, n, a, m, e, ll, pr in two:
                                    dve.wait_ge(S["exp"], n)
                                    dve.tensor_scalar(a, e, -1.0 / 4, 1.0 / 3, ALU.mult, ALU.add)\
                                       .then_inc(S["ser0"], 1)
                                    dve.tensor_scalar(small[ct % 2][:], e, SERIES, None, ALU.is_lt)\
                                       .then_inc(S["small"], 1)
                                for ct, n, a, m, e, ll, pr in two:
                                    dve.wait_ge(S["ser1"], n)
                                    dve.scalar_tensor_tensor(a, a, -0.5, e, ALU.add, ALU.mult).then_inc(S["ser2"], 1)
                                for ct, n, a, m, e, ll, pr in two:
                                    dve.wait_ge(S["ser2"], n)
                                    dve.scalar_tensor_tensor(a, a, 1.0, e, ALU.add, ALU.mult).then_inc(S["ser3"], 1)
                                for ct, n, a, m, e, ll, pr in two:
                                    dve.wait_ge(S["ser3"], n)
                                    dve.wait_ge(S["small"], n)
                                    dve.wait_ge(S["ln"], n)
                                    dve.sem_inc(S["dve_on"], 1)
                                    dve.copy_predicated(ll, small[ct % 2][:], a).then_inc(S["log1p"], 1)
                                for ct, n, a, m, e, ll, pr in two:
                                    dve.wait_ge(S["log1p"], n)
                                    dve.wait_ge(S["relu"], n)
                                    dve.tensor_tensor(m, ll, m, ALU.add).then_inc(S["dt"], 1)
                                for ct, n, a, m, e, ll, pr in two:
                                    dve.wait_ge(S["dt"], n)
                                    dve.wait_ge(S["xc"], n)
                                    dve.tensor_tensor(e, m, xc[:, ct], ALU.mult).then_inc(S["u"], 1)
                                for ct, n, a, m, e, ll, pr in two:
                                    dve.wait_ge(S["u_hi"], n)
                                    dve.tensor_tensor(ll, e, pr[:, 3], ALU.subtract).then_inc(S["u_r"], 1)
                                for ct, n, a, m, e, ll, pr in two:
                                    dve.wait_ge(S["u_mid"], n)
                                    dve.tensor_tensor(pr[:, 5], ll, pr[:, 4], ALU.subtract).then_inc(S["u_parts"], 1)
                            dve.wait_ge(S["bc"], (s + 1) * 2)
                            for ct in range(CT):
                                dve.wait_ge(st_wr[ct], (s + 1) * WR)
                            dve.sem_inc(S["dve_on"], 1)
                            def gate(ct, part):
                                if part == 0:
                                    dve.wait_ge(S["ysum"], (s * CT + ct + 1) * JU)
                                    dve.scalar_tensor_tensor(xc[:, ct], xc[:, ct], W[:, bass.ds(ct + C_DS, 1)],
                                                             flat(6, 2), ALU.mult, ALU.add).then_inc(S["ygate"], 1)
                                else:
                                    dve.wait_ge(S["ygate"], s * CT + ct + 1)
                                    dve.tensor_tensor(sz[:, ct], xc[:, ct], sz[:, ct], ALU.mult)\
                                       .then_inc(S["gated"], 1)

                            def scan_tile(ct, first):
                                n0 = (s * CT + ct) * TU

                                def inject(k):
                                    dve.wait_ge(S["u_rep"], n0 + k + 1)
                                    dve.wait_ge(S["scan"], n0 if first and k < DB else n0 + k - DB + 1)
                                    dve.tensor_tensor(dbu[:, k % DB], flat(4, 2), brep[:], ALU.mult)\
                                       .then_inc(S["dbu"], 1)

                                inject(0)
                                for k in range(TU):
                                    if k + 1 < TU:
                                        inject(k + 1)
                                    dve.wait_ge(S["decay"], n0 + k + 1)
                                    dve.wait_ge(S["dbu"], n0 + k + 1)
                                    dve.wait_ge(S["kept"], n0 if first and k < H else n0 + k - H + 1)
                                    dve.wait_ge(S["hc"], n0 if first and k < H else n0 + k - H + 1)
                                    dve.tensor_tensor_scan(h[:, k % H], flat(2 * (k % 2), 2), dbu[:, k % DB],
                                                           carry[:, c, bass.ds(ct * TU + k, 1)],
                                                           ALU.mult, ALU.add).then_inc(S["scan"], 1)
                                    if not first and k in (QU, QU + 1):
                                        gate(ct - 1, k - QU)

                            scan_tile(0, True)
                            with dve.Fori(1, CT) as ct:
                                scan_tile(ct, False)
                            stats(s + 1, (c + 1) % CHUNKS)
                            normalise(s + 1, (c + 1) % CHUNKS)
                            gate(CT - 1, 0)
                            gate(CT - 1, 1)
                            for i in range(TT):
                                dve.wait_ge(S["o_mm"], s * TT + i + 1)
                                dve.tensor_tensor(xt[:, c, i], PS[:, 4 + i % 4, 0:D], xt[:, c, i], ALU.add)\
                                   .then_inc(S["res"], 1)

            @block.scalar
            def _(act):
                act.wait_ge(S["const"], 64)
                with act.Fori(0, LAYERS) as l:
                    act.wait_ge(S["w_ld"], (l + 1) * 32)
                    act.activation(A[:], W[:, C_A:C_A + UNITS], ACT.Exp).then_inc(S["A_exp"], 1)
                    act.wait_ge(S["A_rdy"], l + 1)
                    with act.Fori(0, BATCH) as b:
                        with act.Fori(0, CHUNKS) as c:
                            s = (l * BATCH + b) * CHUNKS + c
                            for hf in range(2):
                                act.wait_ge(S["tp"], s * 2 + hf + 1)
                                for kt in range(KT):
                                    act.activation(hT[:, kt, hf * HALF:hf * HALF + HALF], PS[:, 2 * hf + kt], ACT.Identity,
                                                   bias=W[:, C_LNB + kt:C_LNB + kt + 1],
                                                   scale=W[:, C_LNW + kt:C_LNW + kt + 1]).then_inc(S["hT"], 1)
                            def conv_in(m):
                                act.wait_ge(S["x_mm"], s * CT + m + 1)
                                act.activation(xp[:, m, DC - 1:], flat(4 + 2 * (m % 2), 2), ACT.Copy)\
                                   .then_inc(S["xp"], 1)

                            conv_in(0)
                            conv_in(1)
                            for m in range(CT):
                                act.wait_ge(S["z_mm"], s * CT + m + 1)
                                act.activation(sz[:, m], flat(2 * (m % 2), 2), ACT.Silu).then_inc(S["sz"], 1)
                                act.wait_ge(S["conv"], s * CT + m + 1)
                                act.activation(xc[:, m], xc[:, m], ACT.Silu).then_inc(S["xc"], 1)
                                if m + 2 < CT:
                                    conv_in(m + 2)
                            act.wait_ge(S["dbl_mm"], s + 1)
                            act.activation(dbl[:], PS[0:R + 2 * NS, 4:6].rearrange("p a t -> p (a t)"),
                                           ACT.Copy).then_inc(S["dbl"], 1)
                            for pair in range(0, CT, 2):
                                two = [(ct, s * CT + ct + 1, *(tmp[ct % 2][:, i] for i in range(4)), prt[ct % 2])
                                       for ct in (pair, pair + 1)]
                                for ct, n, a, m, e, ll, pr in two:
                                    dtb = W[:, C_DTB + ct:C_DTB + ct + 1]
                                    act.wait_ge(S["dt_mm"], n)
                                    if ct >= 2:
                                        act.wait_ge(S["dt_parts"], n - 2)
                                        act.wait_ge(S["u_r"], n - 2)
                                    act.activation(a, flat(2 * (ct % 2), 2), ACT.Abs, bias=dtb).then_inc(S["abs"], 1)
                                    act.activation(m, flat(2 * (ct % 2), 2), ACT.Relu, bias=dtb).then_inc(S["relu"], 1)
                                    act.wait_ge(S["abs"], n)
                                    act.activation(e, a, ACT.Exp, scale=-1.0).then_inc(S["exp"], 1)
                                for ct, n, a, m, e, ll, pr in two:
                                    act.wait_ge(S["exp"], n)
                                    if ct >= 2:
                                        act.wait_ge(S["u_parts"], n - 2)
                                    act.activation(ll, e, ACT.Ln, bias=1.0).then_inc(S["ln"], 1)
                                if pair == 0:
                                    for i, to in enumerate((brep, crep)):
                                        act.wait_ge(S["bc_mm"], s * 2 + i + 1)
                                        act.activation(to[:], flat(6 - 2 * i, 2), ACT.Copy).then_inc(S["bc"], 1)
                                for ct, n, a, m, e, ll, pr in two:
                                    if ct >= 2:
                                        act.wait_ge(st_wr[ct - 2], (s + 1) * WR)
                                    act.wait_ge(S["dt"], n)
                                    act.activation(pr[:, 0], m, ACT.Copy).then_inc(S["dt_hi"], 1)
                                for ct, n, a, m, e, ll, pr in two:
                                    act.wait_ge(S["u"], n)
                                    act.activation(pr[:, 3], e, ACT.Copy).then_inc(S["u_hi"], 1)
                                for ct, n, a, m, e, ll, pr in two:
                                    act.wait_ge(S["dt_r"], n)
                                    act.activation(pr[:, 1], a, ACT.Copy).then_inc(S["dt_mid"], 1)
                                    act.wait_ge(S["u_r"], n)
                                    act.activation(pr[:, 4], ll, ACT.Copy).then_inc(S["u_mid"], 1)

                            def keep(ct, k):
                                act.wait_ge(S["scan"], (s * CT + ct) * TU + k + 1)
                                act.activation(carry[:, 1, bass.ds(ct * TU + k, 1)], h[:, k % H, T - 1:T],
                                               ACT.Copy).then_inc(S["kept"], 1)

                            def decay_tile(ct, first):
                                for k in range(TU):
                                    act.wait_ge(S["dt_rep"], (s * CT + ct) * TU + k + 1)
                                    act.activation(flat(2 * (k % 2), 2), flat(2 * (k % 2), 2), ACT.Exp,
                                                   scale=A[:, bass.ds(ct * TU + k, 1)]).then_inc(S["decay"], 1)
                                    if k >= 2:
                                        keep(ct, k - 2)
                                    elif not first:
                                        keep(ct - 1, TU + k - 2)

                            decay_tile(0, True)
                            with act.Fori(1, CT) as ct:
                                decay_tile(ct, False)
                            keep(CT - 1, TU - 2)
                            keep(CT - 1, TU - 1)

            @block.gpsimd
            def _(pool):
                pool.memset(half[:], -0.5).then_inc(S["half"], 1)
                pool.wait_ge(S["half"], 1)

                def rstd(s):
                    pool.wait_ge(S["ve"], s + 1)
                    pool.tensor_tensor(rs[:], ve[:], half[:], ALU.pow).then_inc(S["rs"], 1)

                rstd(0)
                with pool.Fori(0, LAYERS) as l:
                    with pool.Fori(0, BATCH) as b:
                        with pool.Fori(0, CHUNKS) as c:
                            s = (l * BATCH + b) * CHUNKS + c
                            for pair in range(0, CT, 2):
                                two = [(s * CT + ct + 1, *(tmp[ct % 2][:, i] for i in range(3)), prt[ct % 2])
                                       for ct in (pair, pair + 1)]
                                for n, a, m, e, pr in two:
                                    pool.wait_ge(S["ser0"], n)
                                    pool.tensor_tensor(a, a, e, ALU.mult).then_inc(S["ser1"], 1)
                                for n, a, m, e, pr in two:
                                    pool.wait_ge(S["dt_hi"], n)
                                    pool.tensor_tensor(a, m, pr[:, 0], ALU.subtract).then_inc(S["dt_r"], 1)
                                for n, a, m, e, pr in two:
                                    pool.wait_ge(S["dt_mid"], n)
                                    pool.wait_ge(S["dt_r"], n)
                                    pool.tensor_tensor(pr[:, 2], a, pr[:, 1], ALU.subtract).then_inc(S["dt_parts"], 1)
                            pool.wait_ge(S["bc"], (s + 1) * 2)

                            def output_tile(ct, first):
                                for k in range(TU):
                                    pool.wait_ge(S["scan"], (s * CT + ct) * TU + k + 1)
                                    pool.wait_ge(S["ysum"], (s * CT + ct) * JU + (0 if first and k < HC
                                                                                 else (k - HC) // QU + 1))
                                    pool.tensor_tensor(hc[:, k % HC], h[:, k % H], crep[:], ALU.mult)\
                                        .then_inc(S["hc"], 1)

                            output_tile(0, True)
                            with pool.Fori(1, CT) as ct:
                                output_tile(ct, False)
                            rstd(s + 1)

            @block.tensor
            def _(pe):
                pe.wait_ge(S["const"], 64)

                def to_features(s):
                    for hf in range(2):
                        for i in range(4):
                            pe.wait_ge(S["xh"], s * TT + 4 * hf + i + 1)
                            for kt in range(KT):
                                ins = pe.transpose(PS[:, 2 * hf + kt, i * P:(i + 1) * P],
                                                   xh[:, 4 * hf + i, kt * P:(kt + 1) * P], ident[:])
                        ins.then_inc(S["tp"], 1)

                to_features(0)
                with pe.Fori(0, LAYERS) as l:
                    pe.wait_ge(S["w_ld"], (l + 1) * 32)
                    pe.sem_inc(S["pe_on"], 1)
                    with pe.Fori(0, BATCH) as b:
                        with pe.Fori(0, CHUNKS) as c:
                            s = (l * BATCH + b) * CHUNKS + c
                            def project(m, bank):
                                for hf in range(2):
                                    for kt in range(KT):
                                        ins = pe.matmul(PS[:, bank + hf],
                                                        W[:, C_IN + kt * 2 * DI + m * P:C_IN + kt * 2 * DI + (m + 1) * P],
                                                        hT[:, kt, hf * HALF:(hf + 1) * HALF],
                                                        start=(kt == 0), stop=(kt == KT - 1))
                                return ins

                            def project_x(m):
                                if m >= 2:
                                    pe.wait_ge(S["xp"], s * CT + m - 1)
                                project(m, 4 + 2 * (m % 2)).then_inc(S["x_mm"], 1)

                            def project_z(m):
                                if m >= 2:
                                    pe.wait_ge(S["sz"], s * CT + m - 1)
                                project(CT + m, 2 * (m % 2)).then_inc(S["z_mm"], 1)

                            pe.wait_ge(S["res"], s * TT)
                            pe.wait_ge(S["hT"], (s + 1) * 4)
                            for m in range(CT):
                                project_x(m)
                                if m >= 1:
                                    project_z(m - 1)
                            project_z(CT - 1)
                            pe.wait_ge(S["xp"], (s + 1) * CT)
                            for ct in range(CT):
                                pe.wait_ge(S["xc"], s * CT + ct + 1)
                                for hf in range(2):
                                    ins = pe.matmul(PS[0:R + 2 * NS, 4 + hf],
                                                    W[:, C_XP + ct * (R + 2 * NS):C_XP + (ct + 1) * (R + 2 * NS)],
                                                    xc[:, ct, hf * HALF:(hf + 1) * HALF],
                                                    start=(ct == 0), stop=(ct == CT - 1))
                            ins.then_inc(S["dbl_mm"], 1)
                            pe.wait_ge(S["dbl"], s + 1)
                            pe.wait_ge(S["sz"], (s + 1) * CT)
                            for ct in range(CT):
                                if ct >= 2:
                                    pe.wait_ge(S["relu"], s * CT + ct - 1)
                                for hf in range(2):
                                    ins = pe.matmul(PS[:, 2 * (ct % 2) + hf], DTW[:, ct * P:(ct + 1) * P],
                                                    dbl[0:R, hf * HALF:(hf + 1) * HALF], start=True, stop=True)
                                ins.then_inc(S["dt_mm"], 1)
                                if ct == 1:
                                    for i in range(2):
                                        for hf in range(2):
                                            ins = pe.matmul(PS[:, 6 - 2 * i + hf], selbc[:, i],
                                                            dbl[:, hf * HALF:(hf + 1) * HALF], start=True, stop=True)
                                        ins.then_inc(S["bc_mm"], 1)
                            pe.wait_ge(S["relu"], (s + 1) * CT)
                            pe.wait_ge(S["bc"], (s + 1) * 2)
                            pe.sem_inc(S["pe_on"], 1)

                            def rep_dt(ct, n0, k, first):
                                pe.wait_ge(S["scan"], n0 if first and k < 2 else n0 + k - 1)
                                for hf in range(2):
                                    ins = pe.matmul(flat(2 * (k % 2), 2)[:, hf * HALF:(hf + 1) * HALF], selj[:, k // QU],
                                                    stk[:, ct % 2, 0, k % QU, hf * HALF:(hf + 1) * HALF],
                                                    start=True, stop=True)
                                ins.then_inc(S["dt_rep"], 1)

                            def rep_u(ct, n0, k):
                                pe.wait_ge(S["dbu"], n0 + k)
                                for hf in range(2):
                                    ins = pe.matmul(flat(4, 2)[:, hf * HALF:(hf + 1) * HALF], selj[:, k // QU],
                                                    stk[:, ct % 2, 1, k % QU, hf * HALF:(hf + 1) * HALF],
                                                    start=True, stop=True)
                                ins.then_inc(S["u_rep"], 1)

                            def sum_states(n0, j, hf):
                                pe.wait_ge(S["hc"], n0 + QU * (j + 1))
                                for q in range(QU):
                                    ins = pe.matmul(PS[GC * q:GC * (q + 1), 6 + hf], sely[:, j],
                                                    hc[:, (QU * j + q) % HC, hf * HALF:(hf + 1) * HALF],
                                                    start=(j == 0), stop=(j == JU - 1))
                                if hf:
                                    ins.then_inc(S["ysum"], 1)

                            def states_tile(ct, first):
                                n0 = (s * CT + ct) * TU
                                pe.wait_ge(S["st_ld"], (s * CT + ct + 1) * 32)
                                for k in range(TU):
                                    rep_u(ct, n0, k)
                                    rep_dt(ct, n0, k, first)
                                    if k % QU >= 2 and (k > QU or not first):
                                        if k == QU + 2:
                                            pe.wait_ge(S["ygate"], s * CT + ct)
                                        j, hf = (k // QU - 1) % JU, k % QU - 2
                                        sum_states(n0 if k > QU else n0 - TU, j, hf)

                            states_tile(0, True)
                            with pe.Fori(1, CT) as ct:
                                states_tile(ct, False)
                            for hf in range(2):
                                sum_states((s + 1) * UNITS - TU, JU - 1, hf)
                            pe.wait_ge(S["scan"], (s + 1) * UNITS)
                            to_features(s + 1)
                            pe.wait_ge(S["gated"], (s + 1) * CT)
                            for i in range(TT):
                                if i >= 4:
                                    pe.wait_ge(S["res"], s * TT + i - 3)
                                for ct in range(CT):
                                    ins = pe.matmul(PS[:, 4 + i % 4, 0:D], sz[:, ct, i * P:(i + 1) * P],
                                                    W[:, C_OUT + ct * D:C_OUT + (ct + 1) * D],
                                                    start=(ct == 0), stop=(ct == CT - 1))
                                ins.then_inc(S["o_mm"], 1)
        signals.clear()


SL = 64
HD = 128
TOPK = 8
F_W1 = 0
F_W2 = F_W1 + 2 * KT * HD
F_IH = F_W2 + SL
F_HH = F_IH + KT * 3 * D
F_WV = F_HH + KT * 3 * D
F_WO = F_WV + KT * D
F_B1 = F_WO + KT * D
F_BV = F_B1 + 1
F_SI = F_BV + KT
F_SC = F_SI + D
F_TAU = F_SC + 1
F_ALL = F_TAU + 1
B_B2 = 0
B_IH = B_B2 + SL
B_HH = B_IH + 3 * D
B_BO = B_HH + 3 * D
B_ALL = B_BO + D


def slots(nc, tag, x, out, pack, rows, ident_in):
    TG = 8
    GB = 2
    G = BATCH * GB
    xv = x.rearrange("(g i p) d -> g p i d", i=TG, p=P)
    ov = out.rearrange("(g i p) d -> g p i d", i=TG, p=P)
    with ExitStack() as ctx:
        sb = lambda n, s, d=F32: ctx.enter_context(nc.sbuf_tensor(tag + n, s, d))
        W = sb("weights", [P, F_ALL])
        RB = sb("bias_rows", [1, B_ALL])
        ident = sb("ident", [P, P])
        ones = sb("ones", [1, P])
        half = sb("minushalf", [P, TG])
        S0 = sb("slots", [P, D])
        S0T = sb("slots_feat", [P, KT, P])
        mean = sb("slot_mean", [P, KT])
        c1 = sb("hidden_bias", [P, 1])
        rt = sb("temperature", [P, 4])
        xg = [sb(f"x{k}", [P, TG, D]) for k in range(GB)]
        st = sb("stats", [P, TG, 6])
        mv = sb("meanvar", [P, TG, 2])
        ve = sb("vareps", [P, TG])
        rs = sb("rstd", [P, TG])
        xn = [sb(f"xn{k}", [P, TG, D + 1]) for k in range(GB)]
        xnT = sb("xn_feat", [P, KT, TG * P])
        hT = sb("hidden_feat", [P, TG * P])
        lg = sb("logits", [P, TG, SL])
        top = sb("top8", [P, TG, TOPK])
        rest = sb("logits_without_top", [P, TG, SL])
        sel = sb("chosen", [P, TG, SL])
        ex = sb("exps", [P, TG, SL])
        es = sb("exp_sums", [P, 2, TG])
        al = [sb(f"alpha{k}", [P, TG, SL]) for k in range(GB)]
        aT = sb("alpha_feat", [SL + 1, G * TG, P])
        ws = sb("slot_weight", [SL, BATCH, 1])
        gi = sb("slot_input", [SL, BATCH, D])
        giT = sb("slot_input_feat", [P, KT, BATCH, SL])
        rz = sb("gates", [P, 2 * D])
        hn = sb("candidate", [P, 3, D])
        S1 = sb("new_slots", [P, D])
        S1T = sb("new_slots_feat", [P, KT, P])
        SVT = sb("slot_values_feat", [P, KT, P])
        SVo = sb("slot_out", [SL + 1, BATCH, D])
        yo = [sb(f"y{k}", [P, TG, D]) for k in range(GB)]
        PS = ctx.enter_context(nc.psum_tensor(tag + "psum", [P, 8, HALF], F32))
        names = ("w_ld half one_row ones slots s_tp s_feat mean c_mm c1 rt x_ld ve rs xn tp xnT h_mm hT l_mm lg top rest "
                 "chosen shift ex alpha a_tp aT slot_mm ws gi g_tp giT g_mm hn_mm rz_s hn n1 n2 n_t S1 s1_tp S1T sv_mm SVT "
                 "so_mm SVo o_mm y dve dve_on pe_on").split()
        signals = Signals(nc)
        S = {n: signals.add(tag + n) for n in names}
        ld = [signals.add(f"{tag}x_loaded{k}") for k in range(GB)]
        ld2 = [signals.add(f"{tag}x_loaded_again{k}") for k in range(GB)]
        stored = [signals.add(f"{tag}stored{k}") for k in range(GB)]
        with nc.Block() as block:
            @block.sync
            def _(sp):
                sp.dma_start(W[:], pack).then_inc(S["w_ld"], 16)
                sp.dma_start(RB[:], rows).then_inc(S["w_ld"], 16)
                sp.dma_start(ident[:], ident_in).then_inc(S["w_ld"], 16)
                sp.dma_start(SVo[SL:SL + 1, 0], rows[:, B_BO:B_ALL]).then_inc(S["w_ld"], 16)
                sp.dma_start(SVo[SL:SL + 1, 1], rows[:, B_BO:B_ALL]).then_inc(S["w_ld"], 16)
                with sp.Fori(0, BATCH) as b:
                    for k in range(GB):
                        g = b * GB + k
                        sp.wait_ge(S["xn"], b * GB + k - 1 if k else b * GB)
                        sp.dma_start(xg[k][:], xv[g]).then_inc(ld[k], 16)
                for g in range(GB):
                    sp.wait_ge(S["xn"], G)
                    sp.dma_start(xg[g][:], xv[g]).then_inc(ld2[g], 16)
                for g in range(G):
                    k = g % GB
                    sp.wait_ge(S["y"], (g + 1) * TG)
                    sp.dma_start(ov[g], yo[k][:]).then_inc(stored[k], 16)
                    if g + GB < G:
                        sp.dma_start(xg[k][:], xv[g + GB]).then_inc(ld2[k], 16)
                for k in range(GB):
                    sp.wait_ge(stored[k], 16 * G // GB)

            @block.gpsimd
            def _(pool):
                pool.memset(half[:], -0.5).then_inc(S["half"], 1)
                pool.memset(ones[:], 1.0).then_inc(S["ones"], 1)
                pool.memset(xn[0][:, :, D:], 1.0).then_inc(S["ones"], 1)
                pool.memset(xn[1][:, :, D:], 1.0).then_inc(S["ones"], 1)
                pool.wait_ge(S["half"], 1)
                with pool.Fori(0, G) as g:
                    pool.wait_ge(S["ve"], g + 1)
                    pool.tensor_tensor(rs[:], ve[:], half[:], ALU.pow).then_inc(S["rs"], 1)

            @block.vector
            def _(dve):
                dve.memset(aT[SL:SL + 1], 1.0).then_inc(S["one_row"], 1)
                dve.wait_ge(S["w_ld"], 80)
                dve.tensor_scalar(S0[:], W[:, F_SI:F_SI + D], W[:, F_SC:F_SC + 1], None, ALU.mult).then_inc(S["slots"], 1)
                dve.tensor_scalar(rt[:, 0:1], W[:, F_TAU:F_TAU + 1], -1.0, None, ALU.mult).then_inc(S["rt"], 1)
                dve.wait_ge(S["rt"], 1)
                dve.tensor_tensor(rt[:, 1:2], rt[:, 0:1], W[:, F_TAU:F_TAU + 1], ALU.max).then_inc(S["rt"], 1)
                dve.wait_ge(S["rt"], 2)
                dve.tensor_scalar(rt[:, 2:3], rt[:, 1:2], 0.1, None, ALU.add).then_inc(S["rt"], 1)
                dve.wait_ge(S["rt"], 3)
                dve.reciprocal(rt[:, 3:4], rt[:, 2:3]).then_inc(S["rt"], 1)
                dve.wait_ge(S["s_feat"], 1)
                dve.tensor_reduce(mean[:], S0T[:, :, 0:SL], AX, ALU.add).then_inc(S["mean"], 1)
                dve.wait_ge(S["mean"], 1)
                dve.tensor_scalar(mean[:], mean[:], 1.0 / SL, None, ALU.mult).then_inc(S["mean"], 1)
                dve.wait_ge(S["c_mm"], 1)
                dve.tensor_tensor(c1[:], PS[:, 5, 0:1], W[:, F_B1:F_B1 + 1], ALU.add).then_inc(S["c1"], 1)
                PER = 5 * TG + 3
                with dve.Fori(0, BATCH) as b:
                    for k in range(GB):
                        g = b * GB + k
                        own = Chain(dve, S["dve"], g * PER)
                        dve.wait_ge(ld[k], (b + 1) * 16)
                        for i in range(TG):
                            own.add(dve.bn_stats(st[:, i], xg[k][:, i]))
                        own.wait()
                        dve.sem_inc(S["dve_on"], 1)
                        for i in range(TG):
                            own.add(dve.bn_aggr(mv[:, i], st[:, i]))
                        own.wait()
                        dve.tensor_scalar(ve[:], mv[:, :, 1], EPS, None, ALU.add).then_inc(S["ve"], 1)
                        dve.wait_ge(S["rs"], g + 1)
                        dve.wait_ge(S["ones"], 3)
                        dve.wait_ge(S["slot_mm"], b * GB + k - 1 if k else b * GB)
                        for i in range(TG):
                            ins = dve.tensor_scalar(xn[k][:, i, 0:D], xg[k][:, i], mv[:, i, 0:1], rs[:, i:i + 1],
                                                    ALU.subtract, ALU.mult)
                            if i < TG - 1:
                                own.add(ins)
                        ins.then_inc(S["xn"], 1)
                        dve.wait_ge(S["l_mm"], g + 1)
                        dve.tensor_scalar(lg[:].rearrange("p i s -> p (i s)"), PS[:, 6], rt[:, 3:4], None, ALU.mult)\
                            .then_inc(S["lg"], 1)
                        dve.wait_ge(S["lg"], g + 1)
                        dve.sem_inc(S["dve_on"], 1)
                        for i in range(TG):
                            own.add(dve.max(top[:, i], lg[:, i]))
                        own.wait()
                        dve.sem_inc(S["dve_on"], 1)
                        for i in range(TG):
                            own.add(dve.match_replace(rest[:, i], top[:, i], lg[:, i], NEG))
                        dve.tensor_tensor(ex[:], lg[:], top[:, :, 0:1].to_broadcast([P, TG, SL]), ALU.subtract)\
                            .then_inc(S["shift"], 1)
                        own.wait()
                        own.link(dve.tensor_tensor(sel[:], lg[:], rest[:], ALU.not_equal))
                        dve.wait_ge(S["ex"], g + 1)
                        own.link(dve.tensor_tensor(ex[:], ex[:], sel[:], ALU.mult))
                        own.link(dve.tensor_reduce(es[:, 0], ex[:], AX, ALU.add))
                        own.link(dve.reciprocal(es[:, 1], es[:, 0]))
                        dve.tensor_tensor(al[k][:], ex[:], es[:, 1].rearrange("p (i o) -> p i o", o=1).to_broadcast([P, TG, SL]),
                                          ALU.mult).then_inc(S["alpha"], 1)
                        if k == GB - 1:
                            dve.wait_ge(S["slot_mm"], g + 1)
                            dve.tensor_scalar(ws[:, 0], PS[0:SL, 7, D:D + 1], 1e-8, None, ALU.add).then_inc(S["ws"], 1)
                            dve.wait_ge(S["ws"], b * 2 + 1)
                            dve.reciprocal(ws[:, 1], ws[:, 0]).then_inc(S["ws"], 1)
                            dve.wait_ge(S["ws"], b * 2 + 2)
                            dve.tensor_scalar(gi[:, b], PS[0:SL, 7, 0:D], ws[:, 1], None, ALU.mult).then_inc(S["gi"], 1)
                        assert own.n == PER, (own.n, PER)
                dve.wait_ge(S["rz_s"], 1)
                dve.wait_ge(S["hn"], 1)
                dve.tensor_tensor(hn[:, 1], hn[:, 0], rz[:, 0:D], ALU.mult).then_inc(S["n1"], 1)
                dve.wait_ge(S["n1"], 1)
                dve.wait_ge(S["g_mm"], 1)
                dve.tensor_tensor(hn[:, 1], PS[:, 2, 0:D], hn[:, 1], ALU.add).then_inc(S["n2"], 1)
                dve.wait_ge(S["n_t"], 1)
                dve.tensor_tensor(hn[:, 0], S0[:], hn[:, 2], ALU.subtract).then_inc(S["S1"], 1)
                dve.wait_ge(S["S1"], 1)
                dve.tensor_tensor(hn[:, 0], hn[:, 0], rz[:, D:], ALU.mult).then_inc(S["S1"], 1)
                dve.wait_ge(S["S1"], 2)
                dve.tensor_tensor(S1[:], hn[:, 0], hn[:, 2], ALU.add).then_inc(S["S1"], 1)
                dve.wait_ge(S["so_mm"], 1)
                dve.tensor_copy(SVo[0:SL].rearrange("p b d -> p (b d)"), PS[0:SL, 6]).then_inc(S["SVo"], 1)
                for g in range(G):
                    k = g % GB
                    dve.wait_ge(ld2[k], 16 * (g // GB + 1))
                    if g >= GB:
                        dve.wait_ge(stored[k], 16 * (g // GB))
                    for i in range(TG):
                        dve.wait_ge(S["o_mm"], g * TG + i + 1)
                        dve.tensor_tensor(yo[k][:, i], PS[:, i % 4, 0:D], xg[k][:, i], ALU.add).then_inc(S["y"], 1)

            @block.scalar
            def _(act):
                act.wait_ge(S["s_tp"], 1)
                act.activation(S0T[:].rearrange("p k s -> p (k s)"), PS[:, 4, 0:KT * P], ACT.Copy).then_inc(S["s_feat"], 1)
                act.wait_ge(S["c1"], 1)
                act.wait_ge(S["one_row"], 1)
                with act.Fori(0, BATCH) as b:
                    for k in range(GB):
                        g = b * GB + k
                        act.wait_ge(S["tp"], g + 1)
                        for hf in range(2):
                            for kt in range(KT):
                                act.activation(xnT[:, kt, hf * HALF:(hf + 1) * HALF], PS[:, 2 * hf + kt], ACT.Copy)\
                                    .then_inc(S["xnT"], 1)
                        act.wait_ge(S["h_mm"], g + 1)
                        for hf in range(2):
                            act.activation(hT[:, hf * HALF:(hf + 1) * HALF], PS[:, 4 + hf], ACT.Gelu, bias=c1[:])\
                                .then_inc(S["hT"], 1)
                        act.wait_ge(S["shift"], g + 1)
                        act.activation(ex[:], ex[:], ACT.Exp).then_inc(S["ex"], 1)
                        act.wait_ge(S["a_tp"], g + 1)
                        for hf in range(2):
                            act.activation(aT[0:SL, bass.ds(b * (GB * TG) + k * TG + 4 * hf, 4)].rearrange("p i t -> p (i t)"),
                                           PS[0:SL, hf], ACT.Copy).then_inc(S["aT"], 1)
                act.wait_ge(S["g_tp"], 1)
                act.activation(giT[:].rearrange("p k b s -> p (k b s)"), PS[:, 4, 0:KT * BATCH * SL], ACT.Copy)\
                    .then_inc(S["giT"], 1)
                act.wait_ge(S["hn_mm"], 1)
                act.activation(hn[:, 0], PS[:, 1, 0:D], ACT.Copy).then_inc(S["hn"], 1)
                act.wait_ge(S["g_mm"], 1)
                act.activation(rz[:], PS[:, 0], ACT.Sigmoid).then_inc(S["rz_s"], 1)
                act.wait_ge(S["n2"], 1)
                act.activation(hn[:, 2], hn[:, 1], ACT.Tanh).then_inc(S["n_t"], 1)
                act.wait_ge(S["s1_tp"], 1)
                act.activation(S1T[:].rearrange("p k s -> p (k s)"), PS[:, 4, 0:KT * P], ACT.Copy).then_inc(S["S1T"], 1)
                act.wait_ge(S["sv_mm"], 1)
                for kt in range(KT):
                    act.activation(SVT[:, kt], PS[:, 5, kt * P:(kt + 1) * P], ACT.Identity,
                                   bias=W[:, F_BV + kt:F_BV + kt + 1]).then_inc(S["SVT"], 1)

            @block.tensor
            def _(pe):
                pe.wait_ge(S["w_ld"], 80)
                pe.wait_ge(S["slots"], 1)
                for kt in range(KT):
                    ins = pe.transpose(PS[:, 4, kt * P:(kt + 1) * P], S0[:, kt * P:(kt + 1) * P], ident[:])
                ins.then_inc(S["s_tp"], 1)
                pe.wait_ge(S["mean"], 2)
                for kt in range(KT):
                    ins = pe.matmul(PS[:, 5, 0:1], W[:, F_W1 + (KT + kt) * HD:F_W1 + (KT + kt + 1) * HD],
                                    mean[:, kt:kt + 1], start=(kt == 0), stop=(kt == KT - 1))
                ins.then_inc(S["c_mm"], 1)
                pe.wait_ge(S["ones"], 3)
                pe.wait_ge(S["c1"], 1)
                with pe.Fori(0, BATCH) as b:
                    for k in range(GB):
                        g = b * GB + k
                        pe.wait_ge(S["xn"], g + 1)
                        pe.wait_ge(S["aT"], g * 2)
                        for i in range(TG):
                            for kt in range(KT):
                                ins = pe.transpose(PS[:, 2 * (i // 4) + kt, (i % 4) * P:(i % 4 + 1) * P],
                                                   xn[k][:, i, kt * P:(kt + 1) * P], ident[:])
                        ins.then_inc(S["tp"], 1)
                        pe.wait_ge(S["xnT"], (g + 1) * 4)
                        for hf in range(2):
                            for kt in range(KT):
                                ins = pe.matmul(PS[:, 4 + hf], W[:, F_W1 + kt * HD:F_W1 + (kt + 1) * HD],
                                                xnT[:, kt, hf * HALF:(hf + 1) * HALF], start=(kt == 0), stop=(kt == KT - 1))
                        ins.then_inc(S["h_mm"], 1)
                        pe.wait_ge(S["hT"], (g + 1) * 2)
                        pe.wait_ge(S["lg"], g)
                        for i in range(TG):
                            pe.matmul(PS[:, 6, i * SL:(i + 1) * SL], hT[:, i * P:(i + 1) * P], W[:, F_W2:F_W2 + SL],
                                      start=True, stop=False)
                            ins = pe.matmul(PS[:, 6, i * SL:(i + 1) * SL], ones[:], RB[:, B_B2:B_B2 + SL],
                                            start=False, stop=True)
                        ins.then_inc(S["l_mm"], 1)
                        pe.wait_ge(S["alpha"], g + 1)
                        pe.sem_inc(S["pe_on"], 1)
                        for i in range(TG):
                            ins = pe.transpose(PS[0:SL, i // 4, (i % 4) * P:(i % 4 + 1) * P], al[k][:, i], ident[:])
                        ins.then_inc(S["a_tp"], 1)
                        if k == 0:
                            pe.wait_ge(S["gi"], b)
                        for i in range(TG):
                            ins = pe.matmul(PS[0:SL, 7, 0:D + 1], al[k][:, i], xn[k][:, i],
                                            start=(k == 0 and i == 0), stop=(k == GB - 1 and i == TG - 1))
                        ins.then_inc(S["slot_mm"], 1)
                pe.wait_ge(S["gi"], BATCH)
                for kt in range(KT):
                    for b in range(BATCH):
                        at = (kt * BATCH + b) * SL
                        ins = pe.transpose(PS[:, 4, at:at + SL], gi[:, b, kt * P:(kt + 1) * P], ident[0:SL, 0:SL])
                ins.then_inc(S["g_tp"], 1)
                pe.wait_ge(S["aT"], G * 2)
                for kt in range(KT):
                    pe.matmul(PS[:, 1, 0:D], S0T[:, kt], W[:, F_HH + kt * 3 * D + 2 * D:F_HH + (kt + 1) * 3 * D],
                              start=(kt == 0), stop=False)
                pe.matmul(PS[:, 1, 0:D], ones[:], RB[:, B_HH + 2 * D:B_HH + 3 * D], start=False, stop=True)\
                    .then_inc(S["hn_mm"], 1)
                for kt in range(KT):
                    pe.matmul(PS[:, 0], S0T[:, kt], W[:, F_HH + kt * 3 * D:F_HH + kt * 3 * D + 2 * D],
                              start=(kt == 0), stop=False)
                pe.matmul(PS[:, 0], ones[:], RB[:, B_HH:B_HH + 2 * D], start=False, stop=False)
                pe.matmul(PS[:, 0], ones[:], RB[:, B_IH:B_IH + 2 * D], start=False, stop=False)
                pe.wait_ge(S["giT"], 1)
                for kt in range(KT):
                    pe.matmul(PS[:, 0], giT[:, kt].rearrange("p b s -> p (b s)"),
                              W[:, F_IH + kt * 3 * D:F_IH + kt * 3 * D + 2 * D], start=False, stop=(kt == KT - 1))
                for kt in range(KT):
                    pe.matmul(PS[:, 2, 0:D], giT[:, kt].rearrange("p b s -> p (b s)"),
                              W[:, F_IH + kt * 3 * D + 2 * D:F_IH + (kt + 1) * 3 * D], start=(kt == 0), stop=False)
                pe.matmul(PS[:, 2, 0:D], ones[:], RB[:, B_IH + 2 * D:B_IH + 3 * D], start=False, stop=True)\
                    .then_inc(S["g_mm"], 1)
                pe.wait_ge(S["S1"], 3)
                for kt in range(KT):
                    ins = pe.transpose(PS[:, 4, kt * P:(kt + 1) * P], S1[:, kt * P:(kt + 1) * P], ident[:])
                ins.then_inc(S["s1_tp"], 1)
                pe.wait_ge(S["S1T"], 1)
                for mt in range(KT):
                    for kt in range(KT):
                        at = F_WV + kt * D + mt * P
                        ins = pe.matmul(PS[:, 5, mt * P:(mt + 1) * P], W[:, at:at + P], S1T[:, kt],
                                        start=(kt == 0), stop=(kt == KT - 1))
                ins.then_inc(S["sv_mm"], 1)
                pe.wait_ge(S["SVT"], KT)
                for b in range(BATCH):
                    for kt in range(KT):
                        ins = pe.matmul(PS[0:SL, 6, b * D:(b + 1) * D], SVT[:, kt, b * SL:(b + 1) * SL],
                                        W[:, F_WO + kt * D:F_WO + (kt + 1) * D], start=(kt == 0), stop=(kt == KT - 1))
                ins.then_inc(S["so_mm"], 1)
                pe.wait_ge(S["SVo"], 1)
                pe.wait_ge(S["rz_s"], 1)
                for i in range(G * TG):
                    if i >= 4:
                        pe.wait_ge(S["y"], i - 3)
                    pe.matmul(PS[:, i % 4, 0:D], aT[:, i], SVo[:, i // (GB * TG)], start=True, stop=True)\
                        .then_inc(S["o_mm"], 1)
        signals.clear()


NH = 16
HW = D // NH
WIN = 64
HG = NH // 4
FH = P // HW
A_Q = 0
A_K = A_Q + KT * D
A_V = A_K + KT * D
A_P = A_V + KT * D
A_BQ = A_P + KT * D
A_BK = A_BQ + KT
A_HM = A_BK + KT
A_BV = A_HM + FH
A_BP = A_BV + D
A_ALL = A_BP + D


def attention(nc, x, out, pack, mask_in, ident_in, identb_in):
    TG = 4
    C = TG * P
    NC_ = TOK // BATCH // C
    N = BATCH * NC_
    U = TG * HG
    SCALE = 1.0 / 4
    xv = x.rearrange("(g i p) d -> g p i d", i=TG, p=P)
    ov = out.rearrange("(g i p) d -> g p i d", i=TG, p=P)
    with ExitStack() as ctx:
        sb = lambda n, s, d=F32: ctx.enter_context(nc.sbuf_tensor("a_" + n, s, d))
        W = sb("weights", [P, A_ALL])
        ident = sb("ident", [P, P])
        identb = sb("ident_bf16", [P, P], BF16)
        mask = sb("masks", [P, NC_, P], BF16)
        half = sb("minushalf", [P, TG])
        xg = sb("x", [P, 2, TG, D])
        xb = sb("x_bias", [P, 2, TG, D])
        st = sb("stats", [P, TG, 6])
        mv = sb("meanvar", [P, TG, 2])
        ve = sb("vareps", [P, TG])
        rs = sb("rstd", [P, TG])
        xn = sb("xn", [P, TG, D])
        xnT = sb("xn_feat", [P, KT, WIN + C])
        xh = sb("xn_halo", [P, NC_ + 1, KT, WIN])
        bq = sb("q_bias_by_head", [P, KT, FH])
        qS = sb("q_by_head", [P, NH, C])
        kS = sb("k", [P, KT, WIN + C])
        V = sb("v", [P, 2, TG, NH, HW + 1])
        mx = sb("row_max", [P, 2, 4])
        pr = sb("probs", [P, 3, 4, P])
        pT = sb("probs_T", [P, 2, 4, P])
        rc = sb("row_sum_inv", [P, 2, NH])
        y = sb("y", [P, 2, D])
        yT = sb("y_feat", [P, 2, KT, P])
        yo = sb("out", [P, 2, TG, D])
        PS = ctx.enter_context(nc.psum_tensor("a_psum", [P, 8, HALF], F32))
        names = ("const bq half zero vones x_ld ve rs xn tp xnT halo_in halo_out qk_mm qk kh_mm kh v_mm v xb s_mm max "
                 "shift exp p_tp pT av rc y y_tp yT o_mm o dve dve_on").split()
        signals = Signals(nc)
        S = {n: signals.add("a_" + n) for n in names}
        ld = [signals.add(f"a_x_loaded{k}") for k in range(2)]
        stored = [signals.add(f"a_stored{k}") for k in range(2)]
        NU = N * U

        def chunks(eng, body):
            with eng.Fori(0, BATCH) as b:
                with eng.Fori(0, NC_ // 2) as c2:
                    for k in range(2):
                        body((b * (NC_ // 2) + c2) * 2 + k, c2 * 2 + k, k, b * (NC_ // 2) + c2)

        with nc.Block() as block:
            @block.sync
            def _(sp):
                for to, src in ((W, pack), (ident, ident_in), (identb, identb_in), (mask, mask_in)):
                    sp.dma_start(to[:], src).then_inc(S["const"], 16)
                sp.dma_start(xg[:, 0], xv[0]).then_inc(ld[0], 16)

                with sp.Fori(0, N // 2) as s2:
                    for k in range(2):
                        s = s2 * 2 + k
                        sp.wait_ge(S["xb"], s + 1)
                        sp.wait_ge(S["xn"], s + 1)
                        if k == 0:
                            sp.dma_start(xg[:, 1], xv[s + 1]).then_inc(ld[1], 16)
                        else:
                            sp.dma_start(xg[:, 0], xv[(s + 1) % N]).then_inc(ld[0], 16)
                        sp.wait_ge(S["o"], (s + 1) * TG)
                        sp.dma_start(ov[s], yo[:, k]).then_inc(stored[k], 16)
                sp.wait_ge(ld[0], 16 * (N // 2 + 1))
                for k in range(2):
                    sp.wait_ge(stored[k], 16 * N // 2)

            @block.gpsimd
            def _(pool):
                pool.memset(half[:], -0.5).then_inc(S["half"], 1)
                pool.wait_ge(S["half"], 1)
                pool.memset(V[:, :, :, :, HW:], 1.0).then_inc(S["vones"], 1)
                pool.wait_ge(S["const"], 64)

                def body(s, c, k, s2):
                    pool.wait_ge(S["ve"], s + 1)
                    pool.tensor_tensor(rs[:], ve[:], half[:], ALU.pow).then_inc(S["rs"], 1)
                    pool.wait_ge(S["o"], (s2 * 2 + k - 1) * TG if k else s2 * 2 * TG)
                    pool.tensor_tensor(xb[:, k], xg[:, k],
                                       W[:, A_BP:A_BP + D].rearrange("p (o d) -> p o d", o=1).to_broadcast([P, TG, D]),
                                       ALU.add).then_inc(S["xb"], 1)
                chunks(pool, body)

            @block.vector
            def _(dve):
                dve.memset(xh[:, 0], 0.0).then_inc(S["zero"], 1)
                dve.wait_ge(S["zero"], 1)
                dve.wait_ge(S["const"], 64)
                for ft in range(KT):
                    dve.tensor_scalar(bq[:, ft], W[:, A_HM:A_HM + FH], W[:, A_BQ + ft:A_BQ + ft + 1], None, ALU.mult)\
                        .then_inc(S["bq"], 1)
                dve.wait_ge(S["vones"], 1)

                def body(s, c, k, s2):
                    own = Chain(dve, S["dve"], s * 2 * TG)
                    dve.wait_ge(ld[k], 16 * (s2 + 1))
                    for i in range(TG):
                        own.add(dve.bn_stats(st[:, i], xg[:, k, i]))
                    own.wait()
                    dve.sem_inc(S["dve_on"], 1)
                    for i in range(TG):
                        own.add(dve.bn_aggr(mv[:, i], st[:, i]))
                    own.wait()
                    dve.tensor_scalar(ve[:], mv[:, :, 1], EPS, None, ALU.add).then_inc(S["ve"], 1)
                    dve.wait_ge(S["rs"], s + 1)
                    for i in range(TG):
                        ins = dve.tensor_scalar(xn[:, i], xg[:, k, i], mv[:, i, 0:1], rs[:, i:i + 1],
                                                ALU.subtract, ALU.mult)
                    ins.then_inc(S["xn"], 1)
                    dve.wait_ge(S["v_mm"], s * 2 * TG)
                    dve.wait_ge(S["halo_out"], s)
                    dve.sem_inc(S["dve_on"], 1)
                    dve.tensor_copy(xnT[:, :, 0:WIN], xh[:, c]).then_inc(S["halo_in"], 1)
                    dve.wait_ge(S["xnT"], (s + 1) * KT)
                    dve.wait_ge(S["halo_in"], s + 1)
                    dve.tensor_copy(xh[:, c + 1], xnT[:, :, C:]).then_inc(S["halo_out"], 1)
                    for i in range(2 * TG):
                        dve.wait_ge(S["v_mm"], s * 2 * TG + i + 1)
                        dve.tensor_tensor(V[:, i % 2, i // 2, :, 0:HW],
                                          PS[:, 6 + i % 2, 0:D].rearrange("p (h d) -> p h d", h=NH),
                                          W[:, A_BV:A_BV + D].rearrange("p (h d) -> p h d", h=NH), ALU.add)\
                            .then_inc(S["v"], 1)

                    def finish(j):
                        n = s * TG + j + 1
                        dve.wait_ge(S["av"], s * U + (j + 1) * HG)
                        o3 = PS[:, 4 + j % 2, 0:NH * (HW + 1)].rearrange("p (h d) -> p h d", h=NH)
                        dve.reciprocal(rc[:, j % 2], o3[:, :, HW]).then_inc(S["rc"], 1)
                        dve.wait_ge(S["rc"], n)
                        dve.wait_ge(S["y_tp"], n - 2 if j >= 2 else s * TG)
                        dve.tensor_tensor(y[:, j % 2].rearrange("p (h d) -> p h d", h=NH), o3[:, :, 0:HW],
                                          rc[:, j % 2].rearrange("p (h o) -> p h o", o=1).to_broadcast([P, NH, HW]),
                                          ALU.mult).then_inc(S["y"], 1)

                    def add(j):
                        n = s * TG + j + 1
                        dve.wait_ge(S["o_mm"], n)
                        dve.wait_ge(S["xb"], s + 1)
                        dve.tensor_tensor(yo[:, k, j], PS[:, 7, 0:D], xb[:, k, j], ALU.add).then_inc(S["o"], 1)

                    dve.wait_ge(stored[k], 16 * s2)
                    for u in range(U):
                        n = s * U + u + 1
                        dve.wait_ge(S["s_mm"], n)
                        dve.tensor_reduce(mx[:, u % 2], PS[:, u % 2].rearrange("p (h t) -> p h t", h=4), AX, ALU.max)\
                            .then_inc(S["max"], 1)
                        dve.wait_ge(S["max"], n)
                        dve.wait_ge(S["p_tp"], n - 3 if u >= 3 else s * U)
                        dve.tensor_tensor(pr[:, u % 3], PS[:, u % 2].rearrange("p (h t) -> p h t", h=4),
                                          mx[:, u % 2].rearrange("p (h o) -> p h o", o=1).to_broadcast([P, 4, P]),
                                          ALU.subtract).then_inc(S["shift"], 1)
                        if u % HG == 2 and u >= HG:
                            finish(u // HG - 1)
                        if u % HG == 0 and u >= 2 * HG:
                            add(u // HG - 2)
                    finish(TG - 1)
                    add(TG - 2)
                    add(TG - 1)
                chunks(dve, body)

            @block.scalar
            def _(act):
                act.wait_ge(S["const"], 64)
                act.wait_ge(S["bq"], KT)

                def body(s, c, k, s2):
                    act.wait_ge(S["tp"], s + 1)
                    act.wait_ge(S["halo_out"], s)
                    for kt in range(KT):
                        act.activation(xnT[:, kt, WIN:], PS[:, 6 + kt], ACT.Copy).then_inc(S["xnT"], 1)
                    for i in range(2 * KT):
                        ft = i // 2
                        act.wait_ge(S["qk_mm"], s * 2 * KT + i + 1)
                        if i % 2 == 0:
                            for hh in range(FH):
                                ins = act.activation(qS[:, ft * FH + hh], PS[:, 6], ACT.Identity, bias=bq[:, ft, hh:hh + 1],
                                                     scale=W[:, A_HM + hh:A_HM + hh + 1])
                        else:
                            ins = act.activation(kS[:, ft, WIN:], PS[:, 7], ACT.Identity, bias=W[:, A_BK + ft:A_BK + ft + 1])
                        ins.then_inc(S["qk"], 1)

                    act.wait_ge(S["kh_mm"], s + 1)
                    for ft in range(KT):
                        ins = act.activation(kS[:, ft, 0:WIN], PS[:, 5, ft * WIN:(ft + 1) * WIN], ACT.Identity,
                                             bias=W[:, A_BK + ft:A_BK + ft + 1])
                    ins.then_inc(S["kh"], 1)

                    def evac(u):
                        n = s * U + u + 1
                        act.wait_ge(S["p_tp"], n)
                        act.wait_ge(S["av"], n - 2 if u >= 2 else s * U)
                        act.activation(pT[:, u % 2].rearrange("p h t -> p (h t)"), PS[:, 2 + u % 2], ACT.Copy)\
                            .then_inc(S["pT"], 1)

                    def yevac(j):
                        act.wait_ge(S["y_tp"], s * TG + j + 1)
                        act.activation(yT[:, j % 2].rearrange("p k t -> p (k t)"), PS[:, 6, 0:D], ACT.Copy)\
                            .then_inc(S["yT"], 1)

                    for u in range(U):
                        act.wait_ge(S["shift"], s * U + u + 1)
                        act.activation(pr[:, u % 3], pr[:, u % 3], ACT.Exp, scale=SCALE).then_inc(S["exp"], 1)
                        if u >= 1:
                            evac(u - 1)
                        if u % HG == 3 and u >= HG:
                            yevac(u // HG - 1)
                    evac(U - 1)
                    yevac(TG - 1)
                chunks(act, body)

            @block.tensor
            def _(pe):
                pe.wait_ge(S["const"], 64)

                def body(s, c, k, s2):
                    pe.wait_ge(S["xn"], s + 1)
                    pe.wait_ge(S["o"], s * TG)
                    for i in range(TG):
                        for kt in range(KT):
                            ins = pe.transpose(PS[:, 6 + kt, i * P:(i + 1) * P], xn[:, i, kt * P:(kt + 1) * P], ident[:])
                    ins.then_inc(S["tp"], 1)
                    pe.wait_ge(S["xnT"], (s + 1) * KT)
                    pe.wait_ge(S["halo_in"], s + 1)
                    for i in range(2 * KT):
                        ft, isk = i // 2, i % 2
                        if i >= 2:
                            pe.wait_ge(S["qk"], s * 2 * KT + i - 1)
                        w = A_K if isk else A_Q
                        for kt in range(KT):
                            ins = pe.matmul(PS[:, 6 + isk], W[:, w + kt * D + ft * P:w + kt * D + (ft + 1) * P],
                                            xnT[:, kt, WIN:], start=(kt == 0), stop=(kt == KT - 1))
                        ins.then_inc(S["qk_mm"], 1)
                    pe.wait_ge(S["qk"], (s + 1) * 2 * KT)
                    for ft in range(KT):
                        for kt in range(KT):
                            ins = pe.matmul(PS[:, 5, ft * WIN:(ft + 1) * WIN],
                                            W[:, A_K + kt * D + ft * P:A_K + kt * D + (ft + 1) * P],
                                            xnT[:, kt, 0:WIN], start=(kt == 0), stop=(kt == KT - 1))
                    ins.then_inc(S["kh_mm"], 1)
                    for i in range(2 * TG):
                        if i >= 2:
                            pe.wait_ge(S["v"], s * 2 * TG + i - 1)
                        at = (i // 2) * P + (WIN if i % 2 else 0)
                        for kt in range(KT):
                            ins = pe.matmul(PS[:, 6 + i % 2, 0:D], xnT[:, kt, at:at + P],
                                            W[:, A_V + kt * D:A_V + (kt + 1) * D], start=(kt == 0), stop=(kt == KT - 1))
                        ins.then_inc(S["v_mm"], 1)
                    pe.wait_ge(S["v"], (s + 1) * 2 * TG)
                    pe.wait_ge(S["kh"], s + 1)

                    def scores(u):
                        j, g = u // HG, u % HG
                        pe.wait_ge(S["shift"], s * U + u - 1 if u >= 2 else s * U)
                        bank = PS[:, u % 2]
                        m = mask[:, c] if j == 0 else mask[:, 1]
                        pe.matmul(bank.rearrange("p (h t) -> p h t", h=4), identb[:],
                                  m.rearrange("p (o t) -> p o t", o=1).to_broadcast([P, 4, P]), start=True, stop=False)
                        for r in range(4):
                            for blk in range(2):
                                ins = pe.matmul(PS[WIN * blk:WIN * (blk + 1), u % 2, r * P:(r + 1) * P],
                                                qS[:, 4 * g + r, j * P + WIN * blk:j * P + WIN * (blk + 1)],
                                                kS[:, 4 * g // FH, j * P + WIN * blk:j * P + WIN * blk + P],
                                                start=False, stop=(r == 3))
                        ins.then_inc(S["s_mm"], 1)

                    def transp(u):
                        pe.wait_ge(S["exp"], s * U + u + 1)
                        pe.wait_ge(S["pT"], s * U + u - 1 if u >= 2 else s * U)
                        for r in range(4):
                            ins = pe.transpose(PS[:, 2 + u % 2, r * P:(r + 1) * P], pr[:, u % 3, r], ident[:])
                        ins.then_inc(S["p_tp"], 1)

                    def values(u):
                        j, g = u // HG, u % HG
                        pe.wait_ge(S["pT"], s * U + u + 1)
                        if g == 0:
                            pe.wait_ge(S["y"], s * TG + j - 1 if j >= 2 else s * TG)
                        for r in range(4):
                            h = 4 * g + r
                            for blk in range(2):
                                ins = pe.matmul(PS[WIN * blk:WIN * (blk + 1), 4 + j % 2, h * (HW + 1):(h + 1) * (HW + 1)],
                                                pT[:, u % 2, r, WIN * blk:WIN * (blk + 1)], V[:, blk, j, h],
                                                start=True, stop=True)
                        ins.then_inc(S["av"], 1)

                    def ytr(j):
                        n = s * TG + j + 1
                        pe.wait_ge(S["y"], n)
                        pe.wait_ge(S["yT"], n - 1)
                        for kt in range(KT):
                            ins = pe.transpose(PS[:, 6, kt * P:(kt + 1) * P], y[:, j % 2, kt * P:(kt + 1) * P], ident[:])
                        ins.then_inc(S["y_tp"], 1)

                    def project(j):
                        n = s * TG + j + 1
                        pe.wait_ge(S["yT"], n)
                        pe.wait_ge(S["o"], n - 1)
                        for kt in range(KT):
                            ins = pe.matmul(PS[:, 7, 0:D], yT[:, j % 2, kt], W[:, A_P + kt * D:A_P + (kt + 1) * D],
                                            start=(kt == 0), stop=(kt == KT - 1))
                        ins.then_inc(S["o_mm"], 1)

                    for u in range(U + 2):
                        if u < U:
                            scores(u)
                        if u >= 2:
                            values(u - 2)
                        if 1 <= u <= U:
                            transp(u - 1)
                        if u % HG == 3 and HG <= u < U:
                            ytr(u // HG - 1)
                        if u % HG == 0 and 2 * HG <= u < U:
                            project(u // HG - 2)
                    project(TG - 2)
                    ytr(TG - 1)
                    project(TG - 1)
                chunks(pe, body)
        signals.clear()


def hybrid(nc, x, norm_w, packs, dt_w, ident, unit_select, state_sum, bc_select, slot_pack, slot_rows, attn_pack,
           attn_mask, ident_bf16, out):
    scratch = lambda n: nc.dram_tensor(n, [TOK, D], F32, kind="Internal").ap()
    r, x1, x2, x3 = (scratch(n) for n in ("mamba_residual", "after_mamba", "after_slots", "after_attention"))
    first_norm(nc, x, r)
    mamba(nc, r, packs, dt_w, (ident, unit_select, state_sum, bc_select))
    second_norm(nc, x, r, x1, norm_w)
    slots(nc, "f1_", x1, x2, slot_pack, slot_rows, ident)
    attention(nc, x2, x3, attn_pack, attn_mask, ident, ident_bf16)
    slots(nc, "f2_", x3, out, slot_pack, slot_rows, ident)



def mamba_layout(np, a):
    f = lambda n: np.asarray(a["L0_attn_a_" + n])
    per = lambda v, n: v.reshape(n, P).T
    packs = []
    for l in range(LAYERS):
        cols = [f("in_proj_w")[l].T.reshape(KT, P, 2 * DI).transpose(1, 0, 2).reshape(P, -1),
                f("out_proj_w")[l].T.reshape(CT, P, D).transpose(1, 0, 2).reshape(P, -1),
                f("x_proj_w")[l].T.reshape(CT, P, R + 2 * NS).transpose(1, 0, 2).reshape(P, -1),
                f("A_log")[l].reshape(CT, QU, JU, EU, NS).transpose(3, 4, 0, 2, 1).reshape(P, UNITS),
                f("conv_w")[l].reshape(CT, P, DC).transpose(1, 0, 2).reshape(P, -1),
                per(f("conv_b")[l], CT), per(f("dt_proj_b")[l], CT), per(f("D_skip")[l], CT),
                per(f("ln_w")[l], KT), per(f("ln_b")[l], KT)]
        packs.append(np.concatenate(cols, 1))
    m = np.arange(P)
    unit_select = np.zeros((PARTS * GC, JU, P), np.float32)
    state_sum = np.zeros((P, JU, GC), np.float32)
    for j in range(JU):
        for p in range(PARTS):
            unit_select[GC * p + EU * j + m // NS, j, m] = 1
        state_sum[m, j, EU * j + m // NS] = 1
    bc_select = np.zeros((R + 2 * NS, 2, P), np.float32)
    for i in range(2):
        bc_select[R + NS * i + m % NS, i, m] = 1
    return np.stack(packs), np.stack([w.T for w in f("dt_proj_w")]), unit_select, state_sum, bc_select


def by_rows(w):
    return w.reshape(-1, P, w.shape[1]).transpose(1, 0, 2).reshape(P, -1)


def slot_layout(np, a):
    f = lambda n: np.asarray(a["L0_ffn_" + n])
    pack = np.concatenate([by_rows(f("w1").T), f("w2").T, by_rows(f("gru_wih").T), by_rows(f("gru_whh").T),
                           by_rows(f("wv").T), by_rows(f("wo").T), f("b1").reshape(P, 1), f("bv").reshape(KT, P).T,
                           np.tile(f("slot_init"), (2, 1)), np.tile(f("slot_scale"), (2, 1)),
                           np.broadcast_to(f("tau"), (P, 1))], 1)
    return pack, np.concatenate([f("b2"), f("gru_bih"), f("gru_bhh"), f("bo")])[None]


def attention_layout(np, a):
    f = lambda n: np.asarray(a["L0_attn_b_" + n])
    w, b = f("W_qkv"), f("b_qkv")
    heads = (np.arange(P)[:, None] // HW == np.arange(FH)[None]).astype(np.float32)
    pack = np.concatenate([by_rows(w[:, :D]), by_rows(w[:, D:2 * D]), by_rows(w[:, 2 * D:]), by_rows(f("W_proj")),
                           b[:D].reshape(KT, P).T, b[D:2 * D].reshape(KT, P).T, heads,
                           np.broadcast_to(b[2 * D:], (P, D)), np.broadcast_to(f("b_proj"), (P, D))], 1)
    q, k = np.arange(P)[:, None] % WIN, np.arange(P)[None]
    inner = np.where((k > q) & (k <= q + WIN), 0.0, NEG)
    first = inner.copy()
    first[:WIN, :WIN] = NEG
    return pack, np.stack([first, inner, inner, inner], 1)


def kernel(**inputs):
    import ml_dtypes
    import numpy as np
    import concourse.bacc as bacc
    from concourse.bass_utils import run_bass_kernel_spmd

    nc = bacc.Bacc("TRN2", target_bir_lowering=False, num_devices=1)
    bf16 = ml_dtypes.bfloat16
    x = np.asarray(inputs["L0_attn_a_x"])
    packs, dt_w, unit_select, state_sum, bc_select = mamba_layout(np, inputs)
    slot_pack, slot_rows = slot_layout(np, inputs)
    attn_pack, attn_mask = attention_layout(np, inputs)
    ident = np.eye(P, dtype=np.float32)
    norm_w = np.stack([np.broadcast_to(np.asarray(inputs["L0_attn_a_norm_f_" + n]), (P, D)) for n in "wb"], 1)
    given = dict(x=x.reshape(TOK, D), norm_w=norm_w, packs=packs, dt_w=dt_w, ident=ident,
                 unit_select=unit_select.astype(bf16), state_sum=state_sum, bc_select=bc_select, slot_pack=slot_pack,
                 slot_rows=slot_rows, attn_pack=attn_pack, attn_mask=attn_mask.astype(bf16), ident_bf16=ident.astype(bf16))
    arrays, args = {}, []
    for name, a in given.items():
        a = np.ascontiguousarray(a)
        arrays[f"in_{name}_dram"] = a
        args.append(nc.dram_tensor(f"in_{name}_dram", a.shape, mybir.dt.from_np(a.dtype), kind="ExternalInput").ap())
    args.append(nc.dram_tensor("out_dram", [TOK, D], F32, kind="ExternalOutput").ap())
    hybrid(nc, *args)
    got = run_bass_kernel_spmd(nc, [arrays], core_ids=[0])
    return got.results[0]["out_dram"].reshape(x.shape)
```

```python
from contextlib import ExitStack

import concourse.bass as bass
from concourse import mybir

F32 = mybir.dt.float32
BF16 = mybir.dt.bfloat16
ALU = mybir.AluOpType
ACT = mybir.ActivationFunctionType
AX = mybir.AxisListType.X

P = 128
D = 256
KT = D // P
TOK = 4096
EPS = 1e-5
SERIES = 1.0 / 32
NEG = -1.0e30

LAYERS = 2
DI = 512
CT = DI // P
NS = 16
R = 16
DC = 4
T = 1024
TT = T // P
CHUNKS = 2
BATCH = 2
HALF = 512
EU = P // NS
GC = 32
JU = GC // EU
QU = P // GC
UNITS = CT * JU * QU
TU = JU * QU
SLAG = 2
GATE = SLAG + QU - 1
PARTS = 3

XW = 64
C_IN = 0
C_CW = C_IN + KT * 2 * DI
C_CB = C_CW + CT * DC
C_DTB = C_CB + CT
C_LNW = C_DTB + CT
C_LNB = C_LNW + KT
C_ALL = C_LNB + KT
C_OUT = 0
C_XP = C_OUT + CT * D
C_A = C_XP + CT * XW
C_DS = C_A + UNITS
C2_ALL = C_DS + CT




class Signals:

    def __init__(self, nc):
        self.nc, self.held = nc, []

    def add(self, name):
        self.held.append(self.nc.alloc_semaphore(name))
        return self.held[-1]

    def clear(self):
        self.nc.all_engine_barrier()
        self.nc.clear_and_free_semaphores(self.held)
        self.nc.all_engine_barrier()


class Chain:

    def __init__(self, eng, sem, base=0, n=0):
        self.eng, self.sem, self.base, self.n = eng, sem, base, n

    def add(self, ins):
        ins.then_inc(self.sem, 1)
        self.n += 1
        return self.n

    def wait(self, n=None):
        self.eng.wait_ge(self.sem, self.base + (self.n if n is None else n))

    def link(self, ins):
        self.add(ins)
        self.wait()


def first_norm(nc, x, r0):
    TG = 8
    NG = TOK // P // TG
    xv = x.rearrange("(g i p) d -> g p i d", i=TG, p=P)
    rv = r0.rearrange("(g i p) d -> g p i d", i=TG, p=P)
    with ExitStack() as ctx:
        sb = lambda n, s, d=F32: ctx.enter_context(nc.sbuf_tensor(n, s, d))
        signals = Signals(nc)
        sem = signals.add
        xt = sb("n0_x", [P, NG, TG, D])
        st = sb("n0_stats", [P, TG, 6])
        mv = sb("n0_meanvar", [P, NG, TG, 2])
        ve = sb("n0_vareps", [P, NG, TG])
        half = sb("n0_minushalf", [P, TG])
        rs = sb("n0_rstd", [P, NG, TG])
        s_half = sem("n0_half_set")
        s_ld = [sem(f"n0_loaded{g}") for g in range(NG)]
        s_v = sem("n0_vector")
        s_ve = sem("n0_var_ready")
        s_rs = sem("n0_rstd_ready")
        s_n = sem("n0_normed")
        s_st = sem("n0_stored")
        with nc.Block() as block:
            @block.sync
            def _(sp):
                for g in range(NG):
                    sp.dma_start(xt[:, g], xv[g]).then_inc(s_ld[g], 16)
                for g in range(NG):
                    sp.wait_ge(s_n, g + 1)
                    sp.dma_start(rv[g], xt[:, g]).then_inc(s_st, 16)
                sp.wait_ge(s_st, 16 * NG)

            @block.vector
            def _(dve):
                own = Chain(dve, s_v)
                for g in range(NG):
                    dve.wait_ge(s_ld[g], 16)
                    first = own.n
                    for i in range(TG):
                        own.add(dve.bn_stats(st[:, i], xt[:, g, i]))
                    for i in range(TG):
                        own.wait(first + i + 1)
                        own.add(dve.bn_aggr(mv[:, g, i], st[:, i]))
                    own.wait()
                    own.add(dve.tensor_scalar(ve[:, g], mv[:, g, :, 1], EPS, None, ALU.add))
                    own.wait()
                    dve.sem_inc(s_ve, 1)
                    dve.wait_ge(s_rs, g + 1)
                    for i in range(TG):
                        own.add(dve.tensor_scalar(xt[:, g, i], xt[:, g, i], mv[:, g, i, 0:1], rs[:, g, i:i + 1],
                                                  ALU.subtract, ALU.mult))
                    own.wait()
                    dve.sem_inc(s_n, 1)

            @block.gpsimd
            def _(pool):
                pool.memset(half[:], -0.5).then_inc(s_half, 1)
                pool.wait_ge(s_half, 1)
                for g in range(NG):
                    pool.wait_ge(s_ve, g + 1)
                    pool.tensor_tensor(rs[:, g], ve[:, g], half[:], ALU.pow).then_inc(s_rs, 1)
        signals.clear()


def second_norm(nc, x, r, out, norm_in):
    TG = 8
    NG = TOK // P // TG
    xv = x.rearrange("(g i p) d -> g p i d", i=TG, p=P)
    rv = r.rearrange("(g i p) d -> g p i d", i=TG, p=P)
    ov = out.rearrange("(g i p) d -> g p i d", i=TG, p=P)
    with ExitStack() as ctx:
        sb = lambda n, s, d=F32: ctx.enter_context(nc.sbuf_tensor("n1_" + n, s, d))
        signals = Signals(nc)
        sem = lambda n: signals.add("n1_" + n)
        wb = sb("w_b", [P, 2, D])
        xt = sb("x", [P, NG, TG, D])
        rt = sb("r", [P, NG, TG, D])
        st = sb("stats", [P, TG, 6])
        mv = sb("meanvar", [P, NG, TG, 2])
        ve = sb("vareps", [P, NG, TG])
        half = sb("minushalf", [P, TG])
        rs = sb("rstd", [P, NG, TG])
        s_half, s_w, s_v, s_ve, s_rs, s_xb, s_n, s_out, s_st = (
            sem(n) for n in "half_set w_loaded vector var_ready rstd_ready x_bias_ready normed out_ready stored".split())
        s_ld = [sem(f"loaded{g}") for g in range(NG)]
        with nc.Block() as block:
            @block.sync
            def _(sp):
                sp.dma_start(wb[:], norm_in).then_inc(s_w, 16)
                for g in range(NG):
                    sp.dma_start(rt[:, g], rv[g]).then_inc(s_ld[g], 16)
                    sp.dma_start(xt[:, g], xv[g]).then_inc(s_ld[g], 16)
                for g in range(NG):
                    sp.wait_ge(s_out, g + 1)
                    sp.dma_start(ov[g], rt[:, g]).then_inc(s_st, 16)
                sp.wait_ge(s_st, 16 * NG)

            @block.vector
            def _(dve):
                own = Chain(dve, s_v)
                dve.wait_ge(s_w, 16)
                for g in range(NG):
                    first = own.n
                    dve.wait_ge(s_ld[g], 32)
                    for i in range(TG):
                        own.add(dve.bn_stats(st[:, i], rt[:, g, i]))
                    for i in range(TG):
                        own.wait(first + i + 1)
                        own.add(dve.bn_aggr(mv[:, g, i], st[:, i]))
                    own.wait()
                    dve.tensor_scalar(ve[:, g], mv[:, g, :, 1], EPS, None, ALU.add).then_inc(s_ve, 1)
                    dve.wait_ge(s_rs, g + 1)
                    for i in range(TG):
                        own.add(dve.tensor_scalar(rt[:, g, i], rt[:, g, i], mv[:, g, i, 0:1], rs[:, g, i:i + 1],
                                                  ALU.subtract, ALU.mult))
                    own.wait()
                    dve.tensor_tensor(rt[:, g], rt[:, g], wb[:, 0:1].to_broadcast([P, TG, D]), ALU.mult)\
                        .then_inc(s_n, 1)
                    dve.wait_ge(s_n, g + 1)
                    dve.wait_ge(s_xb, g + 1)
                    dve.tensor_tensor(rt[:, g], rt[:, g], xt[:, g], ALU.add).then_inc(s_out, 1)

            @block.gpsimd
            def _(pool):
                pool.memset(half[:], -0.5).then_inc(s_half, 1)
                pool.wait_ge(s_half, 1)
                pool.wait_ge(s_w, 16)
                for g in range(NG):
                    pool.wait_ge(s_ve, g + 1)
                    pool.tensor_tensor(rs[:, g], ve[:, g], half[:], ALU.pow).then_inc(s_rs, 1)
                    pool.wait_ge(s_ld[g], 32)
                    pool.tensor_tensor(xt[:, g], xt[:, g], wb[:, 1:2].to_broadcast([P, TG, D]), ALU.add)\
                        .then_inc(s_xb, 1)
        signals.clear()


def mamba(nc, r, packs, packs2, dtw_in, consts):
    ident_in, selj_in, sely_in, selbc_in = consts
    rv = r.rearrange("(s i p) d -> s p i d", i=TT, p=P)
    stack = nc.dram_tensor("dt_u_stack", [CT, 2, QU, GC, PARTS, T], BF16, kind="Internal").ap()
    with ExitStack() as ctx:
        sb = lambda n, s, d=F32: ctx.enter_context(nc.sbuf_tensor(n, s, d))
        signals = Signals(nc)
        sem = signals.add
        W = sb("weights", [P, C_ALL])
        W2 = sb("weights2", [P, C2_ALL])
        DTW = sb("dt_weights", [P, DI])
        ident = sb("ident", [P, P])
        selj = sb("unit_select", [PARTS * GC, JU, P], BF16)
        sely = sb("state_sum", [P, JU, GC])
        selbc = sb("bc_select", [P, 2, P])
        A = sb("A", [P, UNITS])
        xt = sb("x_tok", [P, CHUNKS, TT, D])
        st = sb("ln_stats", [P, TT, 6])
        mv = sb("ln_meanvar", [P, TT, 2])
        ve = sb("ln_vareps", [P, TT])
        half = sb("minushalf", [P, TT])
        rs = sb("ln_rstd", [P, TT])
        early = sb("exp_for_its_table", [P, 1])
        hT = sb("h_feat", [P, KT, T])
        dbl = sb("dt_B_C", [P, T])
        xp = sb("conv_in", [P, CT, DC - 1 + T])
        halo = sb("conv_halo", [P, CHUNKS + 1, CT, DC - 1])
        xc = sb("conv_out", [P, CT, T])
        sz = sb("silu_z", [P, CT, T])
        brep = sb("B_rep", [P, T])
        crep = sb("C_rep", [P, T])
        stk = sb("stacks", [PARTS * GC, 2, 2, QU, T], BF16)
        small = [sb(f"small_e{k}", [P, T], mybir.dt.uint8) for k in range(2)]
        carry = sb("h_carry", [P, CHUNKS + 1, UNITS])
        H, DB, HC = 4, 4, 8
        ring = sb("ring", [P, H + DB + HC, T])
        h = ring[:, 0:H]
        dbu = ring[:, 7:7 + DB]
        HC_SLOTS = (14, 15, 4, 5, 6, 11, 12, 13)
        hc = lambda k: ring[:, HC_SLOTS[k % HC]]
        xh = ring[:, 0:2].rearrange("p a t -> p (a t)").rearrange("p (i d) -> p i d", d=D)
        tmp = [ring[:, 7 * k:7 * k + 4] for k in range(2)]
        work = [[ring[:, 14 + ct % 2] if i == 2 and ct >= 2 else tmp[ct % 2][:, i] for i in range(4)]
                for ct in range(CT)]
        prt = [ring[:, 7 * k + 4:7 * k + 7].bitcast(BF16).rearrange("p a (b t) -> p (a b) t", t=T) for k in range(2)]
        PS = ctx.enter_context(nc.psum_tensor("psum", [P, 8, HALF], F32))
        flat = lambda a, n: PS[:, a:a + n].rearrange("p a t -> p (a t)")

        names = ("const w1_ld w_ld x_ld st_ld r_st half A_exp A_rdy zero stats ve rs xh tp hT x_mm z_mm xp sz conv xc "
                 "dbl_mm dbl bc_mm bc dt_mm abs relu exp ln ser0 ser1 ser2 ser3 small log1p dt dt_hi dt_r dt_mid "
                 "dt_parts u u_hi u_r u_mid u_parts dt_rep u_rep decay dbu scan kept hc ysum ygate gated o_mm res "
                 "dve dve_on pe_on sp_on").split()
        S = {n: sem("m_" + n) for n in names}
        BY_PART = "q c a t -> (c a) q t"
        st_wr = [sem(f"m_stacks_written{ct}") for ct in range(CT)]
        WR = 2 * 16
        STEPS = BATCH * CHUNKS

        with nc.Block() as block:
            @block.sync
            def _(sp):
                sp.dma_start(xt[:, 0], rv[0]).then_inc(S["x_ld"], 16)
                sp.dma_start(ident[:], ident_in).then_inc(S["const"], 16)
                sp.dma_start(W[:], packs[0]).then_inc(S["w1_ld"], 16)
                sp.dma_start(selj[:], selj_in).then_inc(S["const"], 16)
                sp.dma_start(sely[:], sely_in).then_inc(S["const"], 16)
                sp.dma_start(selbc[:], selbc_in).then_inc(S["const"], 16)
                with sp.Fori(0, LAYERS) as l:
                    sp.wait_ge(S["res"], l * STEPS * TT)
                    sp.sem_inc(S["sp_on"], 1)
                    sp.wait_ge(S["ygate"], l * STEPS * CT)
                    sp.dma_start(W2[:], packs2[l]).then_inc(S["w_ld"], 16)
                    sp.dma_start(DTW[:], dtw_in[l]).then_inc(S["w_ld"], 16)
                    with sp.Fori(0, BATCH) as b:
                        with sp.Fori(0, CHUNKS) as c:
                            bc_ = b * CHUNKS + c
                            s = l * STEPS + bc_
                            sp.wait_ge(S["r_st"], s * 16)
                            sp.wait_ge(S["x_ld"], (s + 1) * 16)
                            sp.dma_start(xt[:, (c + 1) % CHUNKS], rv[(bc_ + 1) % STEPS]).then_inc(S["x_ld"], 16)
                            for ct in range(CT):
                                for te, name in ((0, "dt_parts"), (1, "u_parts")):
                                    if ct == 0 and te == 0:
                                        sp.wait_ge(S["st_ld"], s * CT * 32)
                                        sp.sem_inc(S["sp_on"], 1)
                                        sp.wait_ge(S["u_rep"], s * UNITS)
                                        sp.sem_inc(S["sp_on"], 1)
                                    sp.wait_ge(S[name], s * CT + ct + 1)
                                    sp.dma_start(stack[ct, te].rearrange("q c a t -> (q c) a t"),
                                                 prt[ct % 2][:, PARTS * te:PARTS * te + PARTS]).then_inc(st_wr[ct], 16)
                                if ct == 1:
                                    sp.wait_ge(st_wr[0], (s + 1) * WR)
                                    for te2 in range(2):
                                        sp.dma_start(stk[:, 0, te2], stack[0, te2].rearrange(BY_PART))\
                                            .then_inc(S["st_ld"], 16)
                            for ct in range(1, CT):
                                sp.wait_ge(st_wr[ct], (s + 1) * WR)
                            sp.sem_inc(S["sp_on"], 1)
                            sp.wait_ge(S["relu"], (s + 1) * CT)
                            sp.wait_ge(S["conv"], (s + 1) * CT)
                            sp.wait_ge(S["z_mm"], (s + 1) * CT)
                            sp.dma_start(W[:], packs[(s + 1) // STEPS % LAYERS]).then_inc(S["w1_ld"], 16)
                            with sp.Fori(1, CT) as ct:
                                sp.wait_ge(S["u_rep"], (s * CT + ct - 1) * TU + 1)
                                for te in range(2):
                                    sp.dma_start(stk[:, ct % 2, te], stack[ct, te].rearrange(BY_PART))\
                                        .then_inc(S["st_ld"], 16)
                            sp.wait_ge(S["res"], (s + 1) * TT)
                            sp.dma_start(rv[bc_], xt[:, c]).then_inc(S["r_st"], 16)
                sp.wait_ge(S["r_st"], LAYERS * STEPS * 16)

            @block.vector
            def _(dve):
                for a in (halo, carry):
                    dve.memset(a[:], 0.0).then_inc(S["zero"], 1)

                def stats(s, buf):
                    own = Chain(dve, S["stats"], s * 2 * TT)
                    dve.wait_ge(S["x_ld"], (s + 1) * 16)
                    dve.sem_inc(S["dve_on"], 1)
                    for i in range(TT):
                        own.add(dve.bn_stats(st[:, i], xt[:, buf, i]))
                    own.wait()
                    dve.sem_inc(S["dve_on"], 1)
                    for i in range(TT):
                        own.add(dve.bn_aggr(mv[:, i], st[:, i]))
                    own.wait()
                    dve.tensor_scalar(ve[:], mv[:, :, 1], EPS, None, ALU.add).then_inc(S["ve"], 1)

                def normalise(s, buf, left):
                    dve.wait_ge(S["rs"], s + 1)
                    dve.wait_ge(S["kept"], s * UNITS - left)
                    dve.wait_ge(S["hc"], s * UNITS - left)
                    for i in range(TT):
                        dve.tensor_scalar(xh[:, i], xt[:, buf, i], mv[:, i, 0:1], rs[:, i:i + 1],
                                          ALU.subtract, ALU.mult).then_inc(S["xh"], 1)

                PRE = 2 + CT * (DC - 1)
                chain = lambda s, n: Chain(dve, S["dve"], s * PRE, n)

                def conv(s, m):
                    own = chain(s, 1 + m * (DC - 1))
                    dve.wait_ge(S["xp"], s * CT + m + 1)
                    if m == 0:
                        own.wait()
                    for k in range(DC):
                        w = W[:, C_CW + m * DC + k:C_CW + m * DC + k + 1]
                        if k == 0:
                            ins = dve.tensor_scalar(xc[:, m], xp[:, m, 0:T], w, W[:, C_CB + m:C_CB + m + 1],
                                                    ALU.mult, ALU.add)
                        else:
                            ins = dve.scalar_tensor_tensor(xc[:, m], xp[:, m, k:k + T], w, xc[:, m], ALU.mult, ALU.add)
                        if k < DC - 1:
                            own.add(ins)
                            own.wait()
                        else:
                            ins.then_inc(S["conv"], 1)

                def halo_in(s, c):
                    chain(s, 0).add(dve.tensor_copy(xp[:, :, 0:DC - 1], halo[:, c]))

                stats(0, 0)
                normalise(0, 0, 0)
                dve.wait_ge(S["zero"], 2)
                halo_in(0, 0)
                conv(0, 0)
                conv(0, 1)
                with dve.Fori(0, LAYERS) as l:
                    dve.wait_ge(S["A_exp"], l + 1)
                    dve.tensor_scalar(A[:], A[:], -1.0, None, ALU.mult).then_inc(S["A_rdy"], 1)
                    with dve.Fori(0, BATCH) as b:
                        with dve.Fori(0, CHUNKS) as c:
                            s = (l * BATCH + b) * CHUNKS + c
                            conv(s, 2)
                            conv(s, 3)
                            chain(s, PRE - 1).add(dve.tensor_copy(halo[:, 1], xp[:, :, T:]))
                            for pair in range(0, CT, 2):
                                two = [(ct, s * CT + ct + 1, *work[ct], prt[ct % 2])
                                       for ct in (pair, pair + 1)]
                                for ct, n, a, m, e, ll, pr in two:
                                    dve.wait_ge(S["exp"], n)
                                    if ct >= 2:
                                        dve.wait_ge(S["dt_parts"], n - 2)
                                    dve.tensor_scalar(a, e, -1.0 / 4, 1.0 / 3, ALU.mult, ALU.add)\
                                       .then_inc(S["ser0"], 1)
                                    dve.tensor_scalar(small[ct % 2][:], e, SERIES, None, ALU.is_lt)\
                                       .then_inc(S["small"], 1)
                                for ct, n, a, m, e, ll, pr in two:
                                    dve.wait_ge(S["ser1"], n)
                                    dve.scalar_tensor_tensor(a, a, -0.5, e, ALU.add, ALU.mult).then_inc(S["ser2"], 1)
                                for ct, n, a, m, e, ll, pr in two:
                                    dve.wait_ge(S["ser2"], n)
                                    dve.scalar_tensor_tensor(a, a, 1.0, e, ALU.add, ALU.mult).then_inc(S["ser3"], 1)
                                for ct, n, a, m, e, ll, pr in two:
                                    dve.wait_ge(S["ser3"], n)
                                    dve.wait_ge(S["small"], n)
                                    dve.wait_ge(S["ln"], n)
                                    dve.sem_inc(S["dve_on"], 1)
                                    dve.copy_predicated(ll, small[ct % 2][:], a).then_inc(S["log1p"], 1)
                                for ct, n, a, m, e, ll, pr in two:
                                    dve.wait_ge(S["log1p"], n)
                                    dve.wait_ge(S["relu"], n)
                                    dve.tensor_tensor(m, ll, m, ALU.add).then_inc(S["dt"], 1)
                                for ct, n, a, m, e, ll, pr in two:
                                    dve.wait_ge(S["dt"], n)
                                    dve.wait_ge(S["xc"], n)
                                    dve.tensor_tensor(e, m, xc[:, ct], ALU.mult).then_inc(S["u"], 1)
                                for ct, n, a, m, e, ll, pr in two:
                                    dve.wait_ge(S["u_hi"], n)
                                    dve.tensor_tensor(ll, e, pr[:, 3], ALU.subtract).then_inc(S["u_r"], 1)
                                for ct, n, a, m, e, ll, pr in two:
                                    dve.wait_ge(S["u_mid"], n)
                                    dve.tensor_tensor(pr[:, 5], ll, pr[:, 4], ALU.subtract).then_inc(S["u_parts"], 1)
                            dve.wait_ge(S["bc"], (s + 1) * 2)
                            dve.wait_ge(S["dt_parts"], (s + 1) * CT)
                            dve.sem_inc(S["dve_on"], 1)
                            def gate(ct, part):
                                if part == 0:
                                    dve.wait_ge(S["ysum"], (s * CT + ct + 1) * JU)
                                    dve.scalar_tensor_tensor(xc[:, ct], xc[:, ct], W2[:, bass.ds(ct + C_DS, 1)],
                                                             flat(6, 2), ALU.mult, ALU.add).then_inc(S["ygate"], 1)
                                else:
                                    dve.wait_ge(S["ygate"], s * CT + ct + 1)
                                    dve.tensor_tensor(sz[:, ct], xc[:, ct], sz[:, ct], ALU.mult)\
                                       .then_inc(S["gated"], 1)

                            def scan_tile(ct, first):
                                n0 = (s * CT + ct) * TU

                                def inject(k):
                                    dve.wait_ge(S["u_rep"], n0 + k + 1)
                                    dve.wait_ge(S["scan"], n0 if first and k < DB else n0 + k - DB + 1)
                                    dve.tensor_tensor(dbu[:, k % DB], flat(4, 2), brep[:], ALU.mult)\
                                       .then_inc(S["dbu"], 1)

                                inject(0)
                                for k in range(TU):
                                    if k + 1 < TU:
                                        inject(k + 1)
                                    dve.wait_ge(S["decay"], n0 + k + 1)
                                    dve.wait_ge(S["dbu"], n0 + k + 1)
                                    dve.wait_ge(S["kept"], n0 if first and k < H else n0 + k - H + 1)
                                    dve.wait_ge(S["hc"], n0 if first and k < H else n0 + k - H + 1)
                                    dve.tensor_tensor_scan(h[:, k % H], flat(2 * (k % 2), 2), dbu[:, k % DB],
                                                           carry[:, c, bass.ds(ct * TU + k, 1)],
                                                           ALU.mult, ALU.add).then_inc(S["scan"], 1)
                                    if first and k == QU:
                                        stats(s + 1, (c + 1) % CHUNKS)
                                    if not first and k in (GATE, GATE + 1):
                                        gate(ct - 1, k - GATE)

                            scan_tile(0, True)
                            with dve.Fori(1, CT) as ct:
                                scan_tile(ct, False)
                            normalise(s + 1, (c + 1) % CHUNKS, 2)
                            gate(CT - 1, 0)
                            gate(CT - 1, 1)
                            halo_in(s + 1, (c + 1) % CHUNKS)
                            for m in range(2):
                                conv(s + 1, m)
                                for i in range(m * TT // 2, (m + 1) * TT // 2):
                                    dve.wait_ge(S["o_mm"], s * TT + i + 1)
                                    dve.tensor_tensor(xt[:, c, i], PS[:, i % 4, 0:D], xt[:, c, i], ALU.add)\
                                       .then_inc(S["res"], 1)

            @block.scalar
            def _(act):
                act.wait_ge(S["const"], 64)
                act.wait_ge(S["half"], 1)

                def features(s):
                    act.wait_ge(S["w1_ld"], (s + 1) * 16)
                    for hf in range(2):
                        act.wait_ge(S["tp"], s * 2 + hf + 1)
                        for kt in range(KT):
                            act.activation(hT[:, kt, hf * HALF:hf * HALF + HALF], PS[:, 2 * hf + kt], ACT.Identity,
                                           bias=W[:, C_LNB + kt:C_LNB + kt + 1],
                                           scale=W[:, C_LNW + kt:C_LNW + kt + 1]).then_inc(S["hT"], 1)

                def conv_in(s, m):
                    act.wait_ge(S["x_mm"], s * CT + m + 1)
                    act.activation(xp[:, m, DC - 1:], flat(4 + 2 * (m % 2), 2), ACT.Copy).then_inc(S["xp"], 1)

                features(0)
                conv_in(0, 0)
                conv_in(0, 1)
                with act.Fori(0, LAYERS) as l:
                    act.wait_ge(S["w_ld"], (l + 1) * 32)
                    act.activation(A[:], W2[:, C_A:C_A + UNITS], ACT.Exp).then_inc(S["A_exp"], 1)
                    act.wait_ge(S["A_rdy"], l + 1)
                    with act.Fori(0, BATCH) as b:
                        with act.Fori(0, CHUNKS) as c:
                            s = (l * BATCH + b) * CHUNKS + c

                            def gate_in(m, bank):
                                act.wait_ge(S["z_mm"], s * CT + m + 1)
                                act.activation(sz[:, m], flat(bank, 2), ACT.Silu).then_inc(S["sz"], 1)

                            for m in range(CT):
                                if m in (1, 2):
                                    gate_in(m - 1, 2 * (m - 1))
                                act.wait_ge(S["conv"], s * CT + m + 1)
                                act.activation(xc[:, m], xc[:, m], ACT.Silu).then_inc(S["xc"], 1)
                                if m + 2 < CT:
                                    conv_in(s, m + 2)
                            act.wait_ge(S["dbl_mm"], s + 1)
                            act.activation(dbl[:], flat(4, 2), ACT.Copy).then_inc(S["dbl"], 1)
                            act.activation(early[:], half[:, 0:1], ACT.Exp)

                            def relu(ct, n, m):
                                act.activation(m, flat(2 * (ct % 2), 2), ACT.Relu,
                                               bias=W[:, C_DTB + ct:C_DTB + ct + 1]).then_inc(S["relu"], 1)

                            for ct in range(CT):
                                n, e = s * CT + ct + 1, work[ct][2]
                                act.wait_ge(S["dt_mm"], n)
                                act.activation(e, flat(2 * (ct % 2), 2), ACT.Abs,
                                               bias=W[:, C_DTB + ct:C_DTB + ct + 1]).then_inc(S["abs"], 1)
                                act.wait_ge(S["abs"], n)
                                act.activation(e, e, ACT.Exp, scale=-1.0).then_inc(S["exp"], 1)
                                if ct < 2:
                                    relu(ct, n, work[ct][1])
                            for pair in range(0, CT, 2):
                                two = [(ct, s * CT + ct + 1, *work[ct], prt[ct % 2])
                                       for ct in (pair, pair + 1)]
                                for ct, n, a, m, e, ll, pr in two:
                                    act.wait_ge(S["exp"], n)
                                    if ct >= 2:
                                        act.wait_ge(S["u_parts"], n - 2)
                                    act.activation(ll, e, ACT.Ln, bias=1.0).then_inc(S["ln"], 1)
                                if pair == 2:
                                    for ct, n, a, m, e, ll, pr in two:
                                        act.wait_ge(S["dt_r"], n - 2)
                                        relu(ct, n, m)
                                if pair == 2:
                                    gate_in(2, 6)
                                    gate_in(3, 4)
                                if pair == 0:
                                    for i, to in enumerate((brep, crep)):
                                        act.wait_ge(S["bc_mm"], s * 2 + i + 1)
                                        act.activation(to[:], flat(6 - 2 * i, 2), ACT.Copy).then_inc(S["bc"], 1)
                                for ct, n, a, m, e, ll, pr in two:
                                    if ct >= 2:
                                        act.wait_ge(st_wr[ct - 2], (s + 1) * WR)
                                    act.wait_ge(S["dt"], n)
                                    act.activation(pr[:, 0], m, ACT.Copy).then_inc(S["dt_hi"], 1)
                                for ct, n, a, m, e, ll, pr in two:
                                    act.wait_ge(S["u"], n)
                                    act.activation(pr[:, 3], e, ACT.Copy).then_inc(S["u_hi"], 1)
                                for ct, n, a, m, e, ll, pr in two:
                                    act.wait_ge(S["dt_r"], n)
                                    act.activation(pr[:, 1], a, ACT.Copy).then_inc(S["dt_mid"], 1)
                                    act.wait_ge(S["u_r"], n)
                                    act.activation(pr[:, 4], ll, ACT.Copy).then_inc(S["u_mid"], 1)

                            def keep(ct, k):
                                act.wait_ge(S["scan"], (s * CT + ct) * TU + k + 1)
                                act.activation(carry[:, 1, bass.ds(ct * TU + k, 1)], h[:, k % H, T - 1:T],
                                               ACT.Copy).then_inc(S["kept"], 1)

                            def decay_tile(ct, first):
                                for k in range(TU):
                                    act.wait_ge(S["dt_rep"], (s * CT + ct) * TU + k + 1)
                                    act.activation(flat(2 * (k % 2), 2), flat(2 * (k % 2), 2), ACT.Exp,
                                                   scale=A[:, bass.ds(ct * TU + k, 1)]).then_inc(S["decay"], 1)
                                    if k >= 2:
                                        keep(ct, k - 2)
                                    elif not first:
                                        keep(ct - 1, TU + k - 2)

                            decay_tile(0, True)
                            with act.Fori(1, CT) as ct:
                                decay_tile(ct, False)
                            keep(CT - 1, TU - 2)
                            keep(CT - 1, TU - 1)
                            features(s + 1)
                            conv_in(s + 1, 0)
                            conv_in(s + 1, 1)

            @block.gpsimd
            def _(pool):
                pool.memset(half[:], -0.5).then_inc(S["half"], 1)
                pool.wait_ge(S["half"], 1)

                def rstd(s):
                    pool.wait_ge(S["ve"], s + 1)
                    pool.tensor_tensor(rs[:], ve[:], half[:], ALU.pow).then_inc(S["rs"], 1)

                rstd(0)
                with pool.Fori(0, LAYERS) as l:
                    with pool.Fori(0, BATCH) as b:
                        with pool.Fori(0, CHUNKS) as c:
                            s = (l * BATCH + b) * CHUNKS + c
                            for pair in range(0, CT, 2):
                                two = [(s * CT + ct + 1, *work[ct][:3], prt[ct % 2])
                                       for ct in (pair, pair + 1)]
                                for n, a, m, e, pr in two:
                                    pool.wait_ge(S["ser0"], n)
                                    pool.tensor_tensor(a, a, e, ALU.mult).then_inc(S["ser1"], 1)
                                for n, a, m, e, pr in two:
                                    pool.wait_ge(S["dt_hi"], n)
                                    pool.tensor_tensor(a, m, pr[:, 0], ALU.subtract).then_inc(S["dt_r"], 1)
                                for n, a, m, e, pr in two:
                                    pool.wait_ge(S["dt_mid"], n)
                                    pool.wait_ge(S["dt_r"], n)
                                    pool.tensor_tensor(pr[:, 2], a, pr[:, 1], ALU.subtract).then_inc(S["dt_parts"], 1)
                            pool.wait_ge(S["bc"], (s + 1) * 2)

                            def output_tile(ct, first):
                                for k in range(TU):
                                    if first and HC_SLOTS[k % HC] in (4, 11):
                                        pool.wait_ge(st_wr[CT - 2 if k < QU else CT - 1], (s + 1) * WR)
                                    pool.wait_ge(S["scan"], (s * CT + ct) * TU + k + 1)
                                    pool.wait_ge(S["ysum"], (s * CT + ct) * JU + (0 if first and k < HC
                                                                                 else (k - HC) // QU + 1))
                                    pool.tensor_tensor(hc(k), h[:, k % H], crep[:], ALU.mult)\
                                        .then_inc(S["hc"], 1)
                                    if first and k == QU:
                                        rstd(s + 1)

                            output_tile(0, True)
                            with pool.Fori(1, CT) as ct:
                                output_tile(ct, False)

            @block.tensor
            def _(pe):
                pe.wait_ge(S["const"], 64)

                def to_features(s):
                    for hf in range(2):
                        for i in range(4):
                            pe.wait_ge(S["xh"], s * TT + 4 * hf + i + 1)
                            for kt in range(KT):
                                ins = pe.transpose(PS[:, 2 * hf + kt, i * P:(i + 1) * P],
                                                   xh[:, 4 * hf + i, kt * P:(kt + 1) * P], ident[:])
                        ins.then_inc(S["tp"], 1)

                def project(m, bank):
                    for hf in range(2):
                        for kt in range(KT):
                            ins = pe.matmul(PS[:, bank + hf],
                                            W[:, C_IN + kt * 2 * DI + m * P:C_IN + kt * 2 * DI + (m + 1) * P],
                                            hT[:, kt, hf * HALF:(hf + 1) * HALF],
                                            start=(kt == 0), stop=(kt == KT - 1))
                    return ins

                def project_x(s, m):
                    if m >= 2:
                        pe.wait_ge(S["xp"], s * CT + m - 1)
                    project(m, 4 + 2 * (m % 2)).then_inc(S["x_mm"], 1)

                to_features(0)
                pe.wait_ge(S["w1_ld"], 16)
                pe.wait_ge(S["hT"], 4)
                project_x(0, 0)
                project_x(0, 1)
                with pe.Fori(0, LAYERS) as l:
                    pe.wait_ge(S["w_ld"], (l + 1) * 32)
                    pe.sem_inc(S["pe_on"], 1)
                    with pe.Fori(0, BATCH) as b:
                        with pe.Fori(0, CHUNKS) as c:
                            s = (l * BATCH + b) * CHUNKS + c
                            def project_z(m, bank):
                                project(CT + m, bank).then_inc(S["z_mm"], 1)

                            project_x(s, 2)
                            pe.wait_ge(S["res"], s * TT)
                            project_z(0, 0)
                            project_x(s, 3)
                            project_z(1, 2)
                            pe.wait_ge(S["xp"], (s + 1) * CT)
                            for half in range(2):
                                pe.wait_ge(S["xc"], s * CT + 2 * half + 2)
                                for hf in range(2):
                                    for odd in range(2):
                                        ct = 2 * half + odd
                                        ins = pe.matmul(PS[XW * odd:XW * odd + XW, 4 + hf],
                                                        W2[:, C_XP + ct * XW:C_XP + (ct + 1) * XW],
                                                        xc[:, ct, hf * HALF:(hf + 1) * HALF],
                                                        start=(half == 0), stop=(half == 1))
                            ins.then_inc(S["dbl_mm"], 1)
                            pe.wait_ge(S["dbl"], s + 1)
                            pe.wait_ge(S["sz"], s * CT + 2)
                            for ct in range(CT):
                                if ct >= 2:
                                    pe.wait_ge(S["relu"], s * CT + ct - 1)
                                for hf in range(2):
                                    ins = pe.matmul(PS[:, 2 * (ct % 2) + hf], DTW[:, ct * P:(ct + 1) * P],
                                                    dbl[:, hf * HALF:(hf + 1) * HALF], start=True, stop=True)
                                ins.then_inc(S["dt_mm"], 1)
                            for i in range(2):
                                for hf in range(2):
                                    ins = pe.matmul(PS[:, 6 - 2 * i + hf], selbc[:, i],
                                                    dbl[:, hf * HALF:(hf + 1) * HALF], start=True, stop=True)
                                ins.then_inc(S["bc_mm"], 1)
                            for i in range(2):
                                pe.wait_ge(S["bc"], s * 2 + i + 1)
                                project_z(2 + i, 6 - 2 * i)
                            pe.wait_ge(S["relu"], (s + 1) * CT)
                            pe.wait_ge(S["sz"], (s + 1) * CT)
                            pe.sem_inc(S["pe_on"], 1)

                            def rep_dt(ct, n0, k, first):
                                pe.wait_ge(S["scan"], n0 if first and k < 2 else n0 + k - 1)
                                for hf in range(2):
                                    ins = pe.matmul(flat(2 * (k % 2), 2)[:, hf * HALF:(hf + 1) * HALF], selj[:, k // QU],
                                                    stk[:, ct % 2, 0, k % QU, hf * HALF:(hf + 1) * HALF],
                                                    start=True, stop=True)
                                ins.then_inc(S["dt_rep"], 1)

                            def rep_u(ct, n0, k):
                                pe.wait_ge(S["dbu"], n0 + k)
                                for hf in range(2):
                                    ins = pe.matmul(flat(4, 2)[:, hf * HALF:(hf + 1) * HALF], selj[:, k // QU],
                                                    stk[:, ct % 2, 1, k % QU, hf * HALF:(hf + 1) * HALF],
                                                    start=True, stop=True)
                                ins.then_inc(S["u_rep"], 1)

                            def sum_states(n0, j, part):
                                pe.wait_ge(S["hc"], n0 + QU * (j + 1))
                                at = part * (T // QU)
                                for q in range(QU):
                                    ins = pe.matmul(flat(6, 2)[GC * q:GC * (q + 1), at:at + T // QU], sely[:, j],
                                                    hc(QU * j + q)[:, at:at + T // QU],
                                                    start=(j == 0 and part % 2 == 0),
                                                    stop=(j == JU - 1 and part % 2 == 1))
                                if part == QU - 1:
                                    ins.then_inc(S["ysum"], 1)

                            def states_tile(ct, first):
                                n0 = (s * CT + ct) * TU
                                pe.wait_ge(S["st_ld"], (s * CT + ct + 1) * 32)
                                for k in range(TU):
                                    rep_u(ct, n0, k)
                                    rep_dt(ct, n0, k, first)
                                    j, part = divmod(k - QU - SLAG, QU)
                                    if j >= 0:
                                        if j == 0 and part == 0:
                                            pe.wait_ge(S["ygate"], s * CT + ct)
                                        sum_states(n0, j, part)
                                    elif not first:
                                        sum_states(n0 - TU, j % JU, part)

                            states_tile(0, True)
                            with pe.Fori(1, CT) as ct:
                                states_tile(ct, False)
                            pe.wait_ge(S["scan"], (s + 1) * UNITS)
                            to_features(s + 1)
                            for k in range(TU, TU + QU + SLAG):
                                sum_states((s + 1) * UNITS - TU, *divmod(k - QU - SLAG, QU))
                            pe.wait_ge(S["w1_ld"], (s + 2) * 16)
                            pe.wait_ge(S["hT"], (s + 2) * 4)
                            project_x(s + 1, 0)
                            pe.wait_ge(S["gated"], (s + 1) * CT)
                            for i in range(TT):
                                if i == TT // 2:
                                    project_x(s + 1, 1)
                                if i >= 4:
                                    pe.wait_ge(S["res"], s * TT + i - 3)
                                for ct in range(CT):
                                    ins = pe.matmul(PS[:, i % 4, 0:D], sz[:, ct, i * P:(i + 1) * P],
                                                    W2[:, C_OUT + ct * D:C_OUT + (ct + 1) * D],
                                                    start=(ct == 0), stop=(ct == CT - 1))
                                ins.then_inc(S["o_mm"], 1)
        signals.clear()


SL = 64
HD = 128
TOPK = 8
F_W1 = 0
F_W2 = F_W1 + 2 * KT * HD
F_IH = F_W2 + SL
F_HH = F_IH + KT * 3 * D
F_WV = F_HH + KT * 3 * D
F_WO = F_WV + KT * D
F_B1 = F_WO + KT * D
F_BV = F_B1 + 1
F_SI = F_BV + KT
F_SC = F_SI + D
F_TAU = F_SC + 1
F_ALL = F_TAU + 1
B_B2 = 0
B_IH = B_B2 + SL
B_HH = B_IH + 3 * D
B_BO = B_HH + 3 * D
B_ALL = B_BO + D


def slots(nc, tag, x, out, pack, rows, ident_in):
    TG = 8
    GB = 2
    G = BATCH * GB
    xv = x.rearrange("(g i p) d -> g p i d", i=TG, p=P)
    ov = out.rearrange("(g i p) d -> g p i d", i=TG, p=P)
    with ExitStack() as ctx:
        sb = lambda n, s, d=F32: ctx.enter_context(nc.sbuf_tensor(tag + n, s, d))
        W = sb("weights", [P, F_ALL])
        RB = sb("bias_rows", [1, B_ALL])
        ident = sb("ident", [P, P])
        ones = sb("ones", [1, P])
        half = sb("minushalf", [P, TG])
        S0 = sb("slots", [P, D])
        S0T = sb("slots_feat", [P, KT, P])
        mean = sb("slot_mean", [P, KT])
        c1 = sb("hidden_bias", [P, 1])
        rt = sb("temperature", [P, 4])
        xg = [sb(f"x{k}", [P, TG, D]) for k in range(GB)]
        st = sb("stats", [P, TG, 6])
        mv = sb("meanvar", [P, TG, 2])
        ve = sb("vareps", [P, TG])
        rs = sb("rstd", [P, TG])
        xn = [sb(f"xn{k}", [P, TG, D + 1]) for k in range(GB)]
        xnT = sb("xn_feat", [P, KT, TG * P])
        hT = sb("hidden_feat", [P, TG * P])
        lg = sb("logits", [P, TG, SL])
        top = sb("top8", [P, TG, TOPK])
        rest = sb("logits_without_top", [P, TG, SL])
        sel = sb("chosen", [P, TG, SL])
        ex = sb("exps", [P, TG, SL])
        es = sb("exp_sums", [P, 2, TG])
        al = [sb(f"alpha{k}", [P, TG, SL]) for k in range(GB)]
        aT = sb("alpha_feat", [SL + 1, G * TG, P])
        ws = sb("slot_weight", [SL, BATCH, 1])
        gi = sb("slot_input", [SL, BATCH, D])
        giT = sb("slot_input_feat", [P, KT, BATCH, SL])
        rz = sb("gates", [P, 2 * D])
        hn = sb("candidate", [P, 3, D])
        S1 = sb("new_slots", [P, D])
        S1T = sb("new_slots_feat", [P, KT, P])
        SVT = sb("slot_values_feat", [P, KT, P])
        SVo = sb("slot_out", [SL + 1, BATCH, D])
        yo = [sb(f"y{k}", [P, TG, D]) for k in range(GB)]
        PS = ctx.enter_context(nc.psum_tensor(tag + "psum", [P, 8, HALF], F32))
        names = ("ident w_ld half one_row ones slots s_tp s_feat mean c_mm c1 rt stats ve rs xn tp xnT h_mm hT l_mm lg "
                 "shift ex alpha a_tp aT slot_mm ws gi g_tp giT g_mm hn_mm rz_s hn n1 n2 n_t S1 s1_tp S1T sv_mm "
                 "SVT so_mm SVo o_mm y dve dve_on pe_on").split()
        signals = Signals(nc)
        S = {n: signals.add(tag + n) for n in names}
        ld = [signals.add(f"{tag}x_loaded{k}") for k in range(GB)]
        stored = [signals.add(f"{tag}stored{k}") for k in range(GB)]
        with nc.Block() as block:
            @block.sync
            def _(sp):
                sp.dma_start(xg[0][:], xv[0]).then_inc(ld[0], 16)
                sp.dma_start(ident[:], ident_in).then_inc(S["ident"], 16)
                sp.dma_start(W[:], pack).then_inc(S["w_ld"], 16)
                sp.dma_start(xg[1][:], xv[1]).then_inc(ld[1], 16)
                sp.dma_start(RB[:], rows).then_inc(S["w_ld"], 16)
                sp.dma_start(SVo[SL:SL + 1, 0], rows[:, B_BO:B_ALL]).then_inc(S["w_ld"], 16)
                sp.dma_start(SVo[SL:SL + 1, 1], rows[:, B_BO:B_ALL]).then_inc(S["w_ld"], 16)
                for n in range(GB, G + GB):
                    sp.wait_ge(S["xn"], n - GB + 1)
                    sp.dma_start(xg[n % GB][:], xv[n % G]).then_inc(ld[n % GB], 16)
                for g in range(G):
                    k = g % GB
                    sp.wait_ge(S["y"], (g + 1) * TG)
                    sp.dma_start(ov[g], yo[k][:]).then_inc(stored[k], 16)
                    if g + GB < G:
                        if g == 0:
                            sp.wait_ge(S["xn"], G + 1)
                        sp.dma_start(xg[k][:], xv[g + GB]).then_inc(ld[k], 16)
                for k in range(GB):
                    sp.wait_ge(stored[k], 16 * G // GB)

            @block.gpsimd
            def _(pool):
                pool.memset(half[:], -0.5).then_inc(S["half"], 1)
                pool.memset(ones[:], 1.0).then_inc(S["ones"], 1)
                pool.memset(xn[0][:, :, D:], 1.0).then_inc(S["ones"], 1)
                pool.memset(xn[1][:, :, D:], 1.0).then_inc(S["ones"], 1)
                pool.wait_ge(S["half"], 1)

                def rstd(g):
                    pool.wait_ge(S["ve"], g + 1)
                    pool.tensor_tensor(rs[:], ve[:], half[:], ALU.pow).then_inc(S["rs"], 1)

                rstd(0)
                pool.wait_ge(S["ones"], 3)
                pool.wait_ge(S["rs"], 1)
                pool.memset(aT[SL:SL + 1], 1.0).then_inc(S["one_row"], 1)
                pool.wait_ge(S["one_row"], 1)
                with pool.Fori(1, G + 1) as g:
                    rstd(g)

            @block.vector
            def _(dve):
                def normalise(g, k, loads, summed):
                    own = Chain(dve, S["stats"], g * 2 * TG)
                    dve.wait_ge(ld[k], loads * 16)
                    for i in range(TG):
                        own.add(dve.bn_stats(st[:, i], xg[k][:, i]))
                    own.wait()
                    dve.sem_inc(S["dve_on"], 1)
                    for i in range(TG):
                        own.add(dve.bn_aggr(mv[:, i], st[:, i]))
                    own.wait()
                    dve.tensor_scalar(ve[:], mv[:, :, 1], EPS, None, ALU.add).then_inc(S["ve"], 1)
                    dve.wait_ge(S["rs"], g + 1)
                    dve.wait_ge(S["slot_mm"], summed)
                    for i in range(TG):
                        ins = dve.tensor_scalar(xn[k][:, i, 0:D], xg[k][:, i], mv[:, i, 0:1], rs[:, i:i + 1],
                                                ALU.subtract, ALU.mult)
                    ins.then_inc(S["xn"], 1)

                dve.wait_ge(S["ones"], 3)
                normalise(0, 0, 1, 0)
                dve.wait_ge(S["w_ld"], 64)
                dve.tensor_scalar(S0[:], W[:, F_SI:F_SI + D], W[:, F_SC:F_SC + 1], None, ALU.mult).then_inc(S["slots"], 1)
                dve.tensor_scalar(rt[:, 0:1], W[:, F_TAU:F_TAU + 1], -1.0, None, ALU.mult).then_inc(S["rt"], 1)
                dve.wait_ge(S["rt"], 1)
                dve.tensor_tensor(rt[:, 1:2], rt[:, 0:1], W[:, F_TAU:F_TAU + 1], ALU.max).then_inc(S["rt"], 1)
                dve.wait_ge(S["rt"], 2)
                dve.tensor_scalar(rt[:, 2:3], rt[:, 1:2], 0.1, None, ALU.add).then_inc(S["rt"], 1)
                dve.wait_ge(S["rt"], 3)
                dve.reciprocal(rt[:, 3:4], rt[:, 2:3]).then_inc(S["rt"], 1)
                dve.wait_ge(S["s_feat"], 1)
                dve.tensor_reduce(mean[:], S0T[:, :, 0:SL], AX, ALU.add).then_inc(S["mean"], 1)
                dve.wait_ge(S["mean"], 1)
                dve.tensor_scalar(mean[:], mean[:], 1.0 / SL, None, ALU.mult).then_inc(S["mean"], 1)
                dve.wait_ge(S["c_mm"], 1)
                dve.tensor_tensor(c1[:], PS[:, 5, 0:1], W[:, F_B1:F_B1 + 1], ALU.add).then_inc(S["c1"], 1)
                PER = 2 * TG + 4
                with dve.Fori(0, BATCH) as b:
                    for k in range(GB):
                        g = b * GB + k
                        own = Chain(dve, S["dve"], g * PER)
                        normalise(g + 1, 1 - k, b + 1 + k, g)
                        dve.wait_ge(S["l_mm"], g + 1)
                        dve.tensor_scalar(lg[:].rearrange("p i s -> p (i s)"), PS[:, 6], rt[:, 3:4], None, ALU.mult)\
                            .then_inc(S["lg"], 1)
                        dve.wait_ge(S["lg"], g + 1)
                        dve.sem_inc(S["dve_on"], 1)
                        for i in range(TG):
                            own.add(dve.max(top[:, i], lg[:, i]))
                        own.wait()
                        dve.sem_inc(S["dve_on"], 1)
                        for i in range(TG):
                            own.add(dve.match_replace(rest[:, i], top[:, i], lg[:, i], NEG))
                        dve.tensor_tensor(ex[:], lg[:], top[:, :, 0:1].to_broadcast([P, TG, SL]), ALU.subtract)\
                            .then_inc(S["shift"], 1)
                        own.wait()
                        own.link(dve.tensor_tensor(sel[:], lg[:], rest[:], ALU.not_equal))
                        dve.wait_ge(S["ex"], g + 1)
                        own.link(dve.tensor_tensor(ex[:], ex[:], sel[:], ALU.mult))
                        own.link(dve.tensor_reduce(es[:, 0], ex[:], AX, ALU.add))
                        own.link(dve.reciprocal(es[:, 1], es[:, 0]))
                        dve.tensor_tensor(al[k][:], ex[:], es[:, 1].rearrange("p (i o) -> p i o", o=1).to_broadcast([P, TG, SL]),
                                          ALU.mult).then_inc(S["alpha"], 1)
                        if k == GB - 1:
                            dve.wait_ge(S["slot_mm"], g + 1)
                            dve.tensor_scalar(ws[:, 0], PS[0:SL, 7, D:D + 1], 1e-8, None, ALU.add).then_inc(S["ws"], 1)
                            dve.wait_ge(S["ws"], b * 2 + 1)
                            dve.reciprocal(ws[:, 1], ws[:, 0]).then_inc(S["ws"], 1)
                            dve.wait_ge(S["ws"], b * 2 + 2)
                            dve.tensor_scalar(gi[:, b], PS[0:SL, 7, 0:D], ws[:, 1], None, ALU.mult).then_inc(S["gi"], 1)
                        assert own.n == PER, (own.n, PER)
                dve.wait_ge(S["rz_s"], 1)
                dve.wait_ge(S["hn"], 1)
                dve.tensor_tensor(hn[:, 1], hn[:, 0], rz[:, 0:D], ALU.mult).then_inc(S["n1"], 1)
                dve.wait_ge(S["n1"], 1)
                dve.wait_ge(S["g_mm"], 1)
                dve.tensor_tensor(hn[:, 1], PS[:, 2, 0:D], hn[:, 1], ALU.add).then_inc(S["n2"], 1)
                dve.wait_ge(S["n_t"], 1)
                dve.tensor_tensor(hn[:, 0], S0[:], hn[:, 2], ALU.subtract).then_inc(S["S1"], 1)
                dve.wait_ge(S["S1"], 1)
                dve.tensor_tensor(hn[:, 0], hn[:, 0], rz[:, D:], ALU.mult).then_inc(S["S1"], 1)
                dve.wait_ge(S["S1"], 2)
                dve.tensor_tensor(S1[:], hn[:, 0], hn[:, 2], ALU.add).then_inc(S["S1"], 1)
                dve.wait_ge(S["so_mm"], 1)
                dve.tensor_copy(SVo[0:SL].rearrange("p b d -> p (b d)"), PS[0:SL, 6]).then_inc(S["SVo"], 1)
                for g in range(G):
                    k = g % GB
                    dve.wait_ge(ld[k], 16 * ((G + g) // GB + 1))
                    if g >= GB:
                        dve.wait_ge(stored[k], 16 * (g // GB))
                    for i in range(TG):
                        dve.wait_ge(S["o_mm"], g * TG + i + 1)
                        dve.tensor_tensor(yo[k][:, i], PS[:, i % 4, 0:D], xg[k][:, i], ALU.add).then_inc(S["y"], 1)

            @block.scalar
            def _(act):
                def features(g):
                    act.wait_ge(S["tp"], g + 1)
                    for hf in range(2):
                        for kt in range(KT):
                            act.activation(xnT[:, kt, hf * HALF:(hf + 1) * HALF], PS[:, 2 * hf + kt], ACT.Copy)\
                                .then_inc(S["xnT"], 1)

                features(0)
                act.wait_ge(S["s_tp"], 1)
                act.activation(S0T[:].rearrange("p k s -> p (k s)"), PS[:, 4, 0:KT * P], ACT.Copy).then_inc(S["s_feat"], 1)
                act.wait_ge(S["c1"], 1)
                act.wait_ge(S["one_row"], 1)
                with act.Fori(0, BATCH) as b:
                    for k in range(GB):
                        g = b * GB + k
                        act.wait_ge(S["h_mm"], g + 1)
                        for hf in range(2):
                            act.activation(hT[:, hf * HALF:(hf + 1) * HALF], PS[:, 4 + hf], ACT.Gelu, bias=c1[:])\
                                .then_inc(S["hT"], 1)
                        features(g + 1)
                        act.wait_ge(S["shift"], g + 1)
                        act.activation(ex[:], ex[:], ACT.Exp).then_inc(S["ex"], 1)
                        act.wait_ge(S["a_tp"], g + 1)
                        for hf in range(2):
                            act.activation(aT[0:SL, bass.ds(b * (GB * TG) + k * TG + 4 * hf, 4)].rearrange("p i t -> p (i t)"),
                                           PS[0:SL, 4 + hf], ACT.Copy).then_inc(S["aT"], 1)
                act.wait_ge(S["g_tp"], 1)
                act.activation(giT[:].rearrange("p k b s -> p (k b s)"), PS[:, 4, 0:KT * BATCH * SL], ACT.Copy)\
                    .then_inc(S["giT"], 1)
                act.wait_ge(S["hn_mm"], 1)
                act.activation(hn[:, 0], PS[:, 1, 0:D], ACT.Copy).then_inc(S["hn"], 1)
                act.wait_ge(S["g_mm"], 1)
                act.activation(rz[:], PS[:, 0], ACT.Sigmoid).then_inc(S["rz_s"], 1)
                act.wait_ge(S["n2"], 1)
                act.activation(hn[:, 2], hn[:, 1], ACT.Tanh).then_inc(S["n_t"], 1)
                act.wait_ge(S["s1_tp"], 1)
                act.activation(S1T[:].rearrange("p k s -> p (k s)"), PS[:, 4, 0:KT * P], ACT.Copy).then_inc(S["S1T"], 1)
                act.wait_ge(S["sv_mm"], 1)
                for kt in range(KT):
                    act.activation(SVT[:, kt], PS[:, 5, kt * P:(kt + 1) * P], ACT.Identity,
                                   bias=W[:, F_BV + kt:F_BV + kt + 1]).then_inc(S["SVT"], 1)

            @block.tensor
            def _(pe):
                def features(g, k):
                    pe.wait_ge(S["xn"], g + 1)
                    pe.wait_ge(S["xnT"], g * 4)
                    for i in range(TG):
                        for kt in range(KT):
                            ins = pe.transpose(PS[:, 2 * (i // 4) + kt, (i % 4) * P:(i % 4 + 1) * P],
                                               xn[k][:, i, kt * P:(kt + 1) * P], ident[:])
                    ins.then_inc(S["tp"], 1)

                pe.wait_ge(S["ident"], 16)
                features(0, 0)
                pe.wait_ge(S["w_ld"], 64)
                pe.wait_ge(S["slots"], 1)
                for kt in range(KT):
                    ins = pe.transpose(PS[:, 4, kt * P:(kt + 1) * P], S0[:, kt * P:(kt + 1) * P], ident[:])
                ins.then_inc(S["s_tp"], 1)
                pe.wait_ge(S["mean"], 2)
                for kt in range(KT):
                    ins = pe.matmul(PS[:, 5, 0:1], W[:, F_W1 + (KT + kt) * HD:F_W1 + (KT + kt + 1) * HD],
                                    mean[:, kt:kt + 1], start=(kt == 0), stop=(kt == KT - 1))
                ins.then_inc(S["c_mm"], 1)
                pe.wait_ge(S["ones"], 3)
                pe.wait_ge(S["c1"], 1)
                with pe.Fori(0, BATCH) as b:
                    for k in range(GB):
                        g = b * GB + k
                        pe.wait_ge(S["xnT"], (g + 1) * 4)
                        pe.wait_ge(S["aT"], g * 2)
                        for hf in range(2):
                            for kt in range(KT):
                                ins = pe.matmul(PS[:, 4 + hf], W[:, F_W1 + kt * HD:F_W1 + (kt + 1) * HD],
                                                xnT[:, kt, hf * HALF:(hf + 1) * HALF], start=(kt == 0), stop=(kt == KT - 1))
                        ins.then_inc(S["h_mm"], 1)
                        pe.wait_ge(S["hT"], (g + 1) * 2)
                        pe.wait_ge(S["lg"], g)
                        for i in range(TG):
                            pe.matmul(PS[:, 6, i * SL:(i + 1) * SL], hT[:, i * P:(i + 1) * P], W[:, F_W2:F_W2 + SL],
                                      start=True, stop=False)
                            ins = pe.matmul(PS[:, 6, i * SL:(i + 1) * SL], ones[:], RB[:, B_B2:B_B2 + SL],
                                            start=False, stop=True)
                        ins.then_inc(S["l_mm"], 1)
                        features(g + 1, 1 - k)
                        pe.wait_ge(S["alpha"], g + 1)
                        pe.sem_inc(S["pe_on"], 1)
                        for i in range(TG):
                            ins = pe.transpose(PS[0:SL, 4 + i // 4, (i % 4) * P:(i % 4 + 1) * P], al[k][:, i], ident[:])
                        ins.then_inc(S["a_tp"], 1)
                        if k == 0:
                            pe.wait_ge(S["gi"], b)
                        for i in range(TG):
                            ins = pe.matmul(PS[0:SL, 7, 0:D + 1], al[k][:, i], xn[k][:, i],
                                            start=(k == 0 and i == 0), stop=(k == GB - 1 and i == TG - 1))
                        ins.then_inc(S["slot_mm"], 1)
                pe.wait_ge(S["gi"], BATCH)
                pe.wait_ge(S["aT"], G * 2)
                for kt in range(KT):
                    for b in range(BATCH):
                        at = (kt * BATCH + b) * SL
                        ins = pe.transpose(PS[:, 4, at:at + SL], gi[:, b, kt * P:(kt + 1) * P], ident[0:SL, 0:SL])
                ins.then_inc(S["g_tp"], 1)
                pe.wait_ge(S["xnT"], (G + 1) * 4)
                for kt in range(KT):
                    pe.matmul(PS[:, 1, 0:D], S0T[:, kt], W[:, F_HH + kt * 3 * D + 2 * D:F_HH + (kt + 1) * 3 * D],
                              start=(kt == 0), stop=False)
                pe.matmul(PS[:, 1, 0:D], ones[:], RB[:, B_HH + 2 * D:B_HH + 3 * D], start=False, stop=True)\
                    .then_inc(S["hn_mm"], 1)
                for kt in range(KT):
                    pe.matmul(PS[:, 0], S0T[:, kt], W[:, F_HH + kt * 3 * D:F_HH + kt * 3 * D + 2 * D],
                              start=(kt == 0), stop=False)
                pe.matmul(PS[:, 0], ones[:], RB[:, B_HH:B_HH + 2 * D], start=False, stop=False)
                pe.matmul(PS[:, 0], ones[:], RB[:, B_IH:B_IH + 2 * D], start=False, stop=False)
                pe.wait_ge(S["giT"], 1)
                for kt in range(KT):
                    pe.matmul(PS[:, 0], giT[:, kt].rearrange("p b s -> p (b s)"),
                              W[:, F_IH + kt * 3 * D:F_IH + kt * 3 * D + 2 * D], start=False, stop=(kt == KT - 1))
                for kt in range(KT):
                    pe.matmul(PS[:, 2, 0:D], giT[:, kt].rearrange("p b s -> p (b s)"),
                              W[:, F_IH + kt * 3 * D + 2 * D:F_IH + (kt + 1) * 3 * D], start=(kt == 0), stop=False)
                pe.matmul(PS[:, 2, 0:D], ones[:], RB[:, B_IH + 2 * D:B_IH + 3 * D], start=False, stop=True)\
                    .then_inc(S["g_mm"], 1)
                pe.wait_ge(S["S1"], 3)
                for kt in range(KT):
                    ins = pe.transpose(PS[:, 4, kt * P:(kt + 1) * P], S1[:, kt * P:(kt + 1) * P], ident[:])
                ins.then_inc(S["s1_tp"], 1)
                pe.wait_ge(S["S1T"], 1)
                for mt in range(KT):
                    for kt in range(KT):
                        at = F_WV + kt * D + mt * P
                        ins = pe.matmul(PS[:, 5, mt * P:(mt + 1) * P], W[:, at:at + P], S1T[:, kt],
                                        start=(kt == 0), stop=(kt == KT - 1))
                ins.then_inc(S["sv_mm"], 1)
                pe.wait_ge(S["SVT"], KT)
                for b in range(BATCH):
                    for kt in range(KT):
                        ins = pe.matmul(PS[0:SL, 6, b * D:(b + 1) * D], SVT[:, kt, b * SL:(b + 1) * SL],
                                        W[:, F_WO + kt * D:F_WO + (kt + 1) * D], start=(kt == 0), stop=(kt == KT - 1))
                ins.then_inc(S["so_mm"], 1)
                pe.wait_ge(S["SVo"], 1)
                pe.wait_ge(S["rz_s"], 1)
                for i in range(G * TG):
                    if i >= 4:
                        pe.wait_ge(S["y"], i - 3)
                    pe.matmul(PS[:, i % 4, 0:D], aT[:, i], SVo[:, i // (GB * TG)], start=True, stop=True)\
                        .then_inc(S["o_mm"], 1)
        signals.clear()


NH = 16
HW = D // NH
WIN = 64
HG = NH // 4
FH = P // HW
A_Q = 0
A_K = A_Q + KT * D
A_V = A_K + KT * D
A_P = A_V + KT * D
A_BQ = A_P + KT * D
A_BK = A_BQ + KT
A_HM = A_BK + KT
A_BV = A_HM + FH
A_BP = A_BV + D
A_ALL = A_BP + D


def attention(nc, x, out, pack, mask_in, ident_in, identb_in):
    TG = 4
    C = TG * P
    NC_ = TOK // BATCH // C
    N = BATCH * NC_
    U = TG * HG
    SCALE = 1.0 / 4
    xv = x.rearrange("(g i p) d -> g p i d", i=TG, p=P)
    ov = out.rearrange("(g i p) d -> g p i d", i=TG, p=P)
    with ExitStack() as ctx:
        sb = lambda n, s, d=F32: ctx.enter_context(nc.sbuf_tensor("a_" + n, s, d))
        W = sb("weights", [P, A_ALL])
        ident = sb("ident", [P, P])
        identb = sb("ident_bf16", [P, P], BF16)
        mask = sb("masks", [P, NC_, P], BF16)
        half = sb("minushalf", [P, TG])
        xg = sb("x", [P, 2, TG, D])
        xb = sb("x_bias", [P, 2, TG, D])
        st = sb("stats", [P, TG, 6])
        mv = sb("meanvar", [P, TG, 2])
        ve = sb("vareps", [P, TG])
        rs = sb("rstd", [P, TG])
        xn = sb("xn", [P, TG, D])
        xnT = sb("xn_feat", [P, KT, WIN + C])
        xh = sb("xn_halo", [P, NC_ + 1, KT, WIN])
        bq = sb("q_bias_by_head", [P, KT, FH])
        qS = sb("q_by_head", [P, NH, C])
        kS = sb("k", [P, KT, WIN + C])
        V = sb("v", [P, 2, TG, NH, HW + 1])
        mx = sb("row_max", [P, 2, 4])
        pr = sb("probs", [P, 3, 4, P])
        pT = sb("probs_T", [P, 2, 4, P])
        rc = sb("row_sum_inv", [P, 2, NH])
        y = sb("y", [P, 2, D])
        yT = sb("y_feat", [P, 2, KT, P])
        yo = sb("out", [P, 2, TG, D])
        PS = ctx.enter_context(nc.psum_tensor("a_psum", [P, 8, HALF], F32))
        names = ("const bq half zero vones ve rs xn tp xnT halo_in halo_out q_mm k_mm q_act q_dve k kh_mm kh v_mm v xb s_mm max "
                 "shift exp p_tp pT av rc y y_tp yT o_mm o dve dve_on").split()
        signals = Signals(nc)
        S = {n: signals.add("a_" + n) for n in names}
        ld = [signals.add(f"a_x_loaded{k}") for k in range(2)]
        stored = [signals.add(f"a_stored{k}") for k in range(2)]
        V_BANKS = (2, 0, 1, 3)

        def chunks(eng, body):
            with eng.Fori(0, BATCH) as b:
                with eng.Fori(0, NC_ // 2) as c2:
                    for k in range(2):
                        body((b * (NC_ // 2) + c2) * 2 + k, c2 * 2 + k, k, b * (NC_ // 2) + c2)

        with nc.Block() as block:
            @block.sync
            def _(sp):
                for to, src in ((W, pack), (ident, ident_in), (identb, identb_in), (mask, mask_in)):
                    sp.dma_start(to[:], src).then_inc(S["const"], 16)
                sp.dma_start(xg[:, 0], xv[0]).then_inc(ld[0], 16)

                with sp.Fori(0, N // 2) as s2:
                    for k in range(2):
                        s = s2 * 2 + k
                        sp.wait_ge(S["xb"], s)
                        sp.wait_ge(S["xn"], s)
                        if k == 0:
                            sp.dma_start(xg[:, 1], xv[s + 1]).then_inc(ld[1], 16)
                        else:
                            sp.dma_start(xg[:, 0], xv[(s + 1) % N]).then_inc(ld[0], 16)
                        sp.wait_ge(S["o"], (s + 1) * TG)
                        sp.dma_start(ov[s], yo[:, k]).then_inc(stored[k], 16)
                sp.wait_ge(ld[0], 16 * (N // 2 + 1))
                for k in range(2):
                    sp.wait_ge(stored[k], 16 * N // 2)

            @block.gpsimd
            def _(pool):
                pool.memset(half[:], -0.5).then_inc(S["half"], 1)
                pool.wait_ge(S["half"], 1)
                pool.memset(V[:, :, :, :, HW:], 1.0).then_inc(S["vones"], 1)
                pool.wait_ge(S["const"], 64)

                def prepare(s, k, outputs):
                    pool.wait_ge(S["ve"], s + 1)
                    pool.tensor_tensor(rs[:], ve[:], half[:], ALU.pow).then_inc(S["rs"], 1)
                    pool.wait_ge(S["o"], outputs)
                    pool.tensor_tensor(xb[:, k], xg[:, k],
                                       W[:, A_BP:A_BP + D].rearrange("p (o d) -> p o d", o=1).to_broadcast([P, TG, D]),
                                       ALU.add).then_inc(S["xb"], 1)

                prepare(0, 0, 0)
                chunks(pool, lambda s, c, k, s2: prepare(s + 1, 1 - k, s * TG))

            @block.vector
            def _(dve):
                dve.memset(xh[:, 0], 0.0).then_inc(S["zero"], 1)
                dve.wait_ge(S["zero"], 1)
                dve.wait_ge(S["const"], 64)
                for ft in range(KT):
                    dve.tensor_scalar(bq[:, ft], W[:, A_HM:A_HM + FH], W[:, A_BQ + ft:A_BQ + ft + 1], None, ALU.mult)\
                        .then_inc(S["bq"], 1)
                dve.wait_ge(S["vones"], 1)

                def stats(s, k, loads):
                    own = Chain(dve, S["dve"], s * 2 * TG)
                    dve.wait_ge(ld[k], 16 * loads)
                    for i in range(TG):
                        own.add(dve.bn_stats(st[:, i], xg[:, k, i]))
                    own.wait()
                    dve.sem_inc(S["dve_on"], 1)
                    for i in range(TG):
                        own.add(dve.bn_aggr(mv[:, i], st[:, i]))
                    own.wait()
                    dve.tensor_scalar(ve[:], mv[:, :, 1], EPS, None, ALU.add).then_inc(S["ve"], 1)

                def normalise(s, k):
                    dve.wait_ge(S["rs"], s + 1)
                    dve.wait_ge(S["tp"], s)
                    for i in range(TG):
                        ins = dve.tensor_scalar(xn[:, i], xg[:, k, i], mv[:, i, 0:1], rs[:, i:i + 1],
                                                ALU.subtract, ALU.mult)
                    ins.then_inc(S["xn"], 1)

                stats(0, 0, 1)
                normalise(0, 0)

                def body(s, c, k, s2):
                    dve.wait_ge(S["v_mm"], s * 2 * TG)
                    dve.wait_ge(S["halo_out"], s)
                    dve.sem_inc(S["dve_on"], 1)
                    dve.tensor_copy(xnT[:, :, 0:WIN], xh[:, c]).then_inc(S["halo_in"], 1)
                    dve.wait_ge(S["xnT"], (s + 1) * KT)
                    dve.wait_ge(S["halo_in"], s + 1)
                    dve.tensor_copy(xh[:, c + 1], xnT[:, :, C:]).then_inc(S["halo_out"], 1)
                    dve.wait_ge(S["q_mm"], (s + 1) * KT)
                    for hh in range(FH):
                        ins = dve.tensor_scalar(qS[:, FH + hh], PS[:, 3], W[:, A_HM + hh:A_HM + hh + 1],
                                                bq[:, 1, hh:hh + 1], ALU.mult, ALU.add)
                    ins.then_inc(S["q_dve"], 1)
                    for i in range(2 * TG):
                        dve.wait_ge(S["v_mm"], s * 2 * TG + i + 1)
                        dve.tensor_tensor(V[:, i % 2, i // 2, :, 0:HW],
                                          PS[:, V_BANKS[i % 4], 0:D].rearrange("p (h d) -> p h d", h=NH),
                                          W[:, A_BV:A_BV + D].rearrange("p (h d) -> p h d", h=NH), ALU.add)\
                            .then_inc(S["v"], 1)

                    def finish(j):
                        n = s * TG + j + 1
                        dve.wait_ge(S["av"], s * U + (j + 1) * HG)
                        o3 = PS[:, 4 + j % 2, 0:NH * (HW + 1)].rearrange("p (h d) -> p h d", h=NH)
                        dve.reciprocal(rc[:, j % 2], o3[:, :, HW]).then_inc(S["rc"], 1)
                        dve.wait_ge(S["rc"], n)
                        dve.wait_ge(S["y_tp"], n - 2 if j >= 2 else s * TG)
                        dve.tensor_tensor(y[:, j % 2].rearrange("p (h d) -> p h d", h=NH), o3[:, :, 0:HW],
                                          rc[:, j % 2].rearrange("p (h o) -> p h o", o=1).to_broadcast([P, NH, HW]),
                                          ALU.mult).then_inc(S["y"], 1)

                    def add(j):
                        n = s * TG + j + 1
                        dve.wait_ge(S["o_mm"], n)
                        dve.wait_ge(S["xb"], s + 1)
                        dve.tensor_tensor(yo[:, k, j], PS[:, 7, 0:D], xb[:, k, j], ALU.add).then_inc(S["o"], 1)

                    dve.wait_ge(stored[k], 16 * s2)
                    for u in range(U):
                        n = s * U + u + 1
                        dve.wait_ge(S["s_mm"], n)
                        dve.tensor_reduce(mx[:, u % 2], PS[:, u % 2].rearrange("p (h t) -> p h t", h=4), AX, ALU.max)\
                            .then_inc(S["max"], 1)
                        dve.wait_ge(S["max"], n)
                        dve.wait_ge(S["p_tp"], n - 3 if u >= 3 else s * U)
                        dve.tensor_tensor(pr[:, u % 3], PS[:, u % 2].rearrange("p (h t) -> p h t", h=4),
                                          mx[:, u % 2].rearrange("p (h o) -> p h o", o=1).to_broadcast([P, 4, P]),
                                          ALU.subtract).then_inc(S["shift"], 1)
                        if u % HG == 2 and u >= HG:
                            finish(u // HG - 1)
                        if u % HG == 0 and u >= 2 * HG:
                            add(u // HG - 2)
                        if u == HG + 1:
                            stats(s + 1, 1 - k, s2 + k + 1)
                        if u == 2 * HG + 1:
                            normalise(s + 1, 1 - k)
                    finish(TG - 1)
                    add(TG - 2)
                    add(TG - 1)
                chunks(dve, body)

            @block.scalar
            def _(act):
                act.wait_ge(S["const"], 64)
                act.wait_ge(S["bq"], KT)

                def features(s):
                    act.wait_ge(S["tp"], s + 1)
                    act.wait_ge(S["halo_out"], s)
                    for kt in range(KT):
                        act.activation(xnT[:, kt, WIN:], PS[:, kt], ACT.Copy).then_inc(S["xnT"], 1)

                features(0)

                def body(s, c, k, s2):
                    act.wait_ge(S["q_mm"], s * KT + 1)
                    for hh in range(FH):
                        ins = act.activation(qS[:, hh], PS[:, 2], ACT.Identity, bias=bq[:, 0, hh:hh + 1],
                                             scale=W[:, A_HM + hh:A_HM + hh + 1])
                    ins.then_inc(S["q_act"], 1)
                    for ft in range(KT):
                        act.wait_ge(S["k_mm"], s * KT + ft + 1)
                        act.activation(kS[:, ft, WIN:], PS[:, ft], ACT.Identity, bias=W[:, A_BK + ft:A_BK + ft + 1])\
                            .then_inc(S["k"], 1)

                    act.wait_ge(S["kh_mm"], s + 1)
                    for ft in range(KT):
                        ins = act.activation(kS[:, ft, 0:WIN], PS[:, 4, ft * WIN:(ft + 1) * WIN], ACT.Identity,
                                             bias=W[:, A_BK + ft:A_BK + ft + 1])
                    ins.then_inc(S["kh"], 1)

                    def evac(u):
                        n = s * U + u + 1
                        act.wait_ge(S["p_tp"], n)
                        act.wait_ge(S["av"], n - 2 if u >= 2 else s * U)
                        act.activation(pT[:, u % 2].rearrange("p h t -> p (h t)"), PS[:, 2 + u % 2], ACT.Copy)\
                            .then_inc(S["pT"], 1)

                    def yevac(j):
                        act.wait_ge(S["y_tp"], s * TG + j + 1)
                        act.activation(yT[:, j % 2].rearrange("p k t -> p (k t)"), PS[:, 6, 0:D], ACT.Copy)\
                            .then_inc(S["yT"], 1)

                    for u in range(U):
                        act.wait_ge(S["shift"], s * U + u + 1)
                        act.activation(pr[:, u % 3], pr[:, u % 3], ACT.Exp, scale=SCALE).then_inc(S["exp"], 1)
                        if u >= 1:
                            evac(u - 1)
                        if u % HG == 3 and u >= HG:
                            yevac(u // HG - 1)
                    evac(U - 1)
                    features(s + 1)
                    yevac(TG - 1)
                chunks(act, body)

            @block.tensor
            def _(pe):
                pe.wait_ge(S["const"], 64)

                def features(s):
                    pe.wait_ge(S["xn"], s + 1)
                    pe.wait_ge(S["shift"], s * U)
                    for i in range(TG):
                        for kt in range(KT):
                            ins = pe.transpose(PS[:, kt, i * P:(i + 1) * P], xn[:, i, kt * P:(kt + 1) * P], ident[:])
                    ins.then_inc(S["tp"], 1)

                features(0)

                def body(s, c, k, s2):
                    pe.wait_ge(S["pT"], s * U)
                    pe.wait_ge(S["xnT"], (s + 1) * KT)
                    for i in range(2 * KT):
                        ft, isk = i % KT, i // KT
                        w = A_K if isk else A_Q
                        for kt in range(KT):
                            ins = pe.matmul(PS[:, (2 + i) % 4], W[:, w + kt * D + ft * P:w + kt * D + (ft + 1) * P],
                                            xnT[:, kt, WIN:], start=(kt == 0), stop=(kt == KT - 1))
                        ins.then_inc(S["k_mm" if isk else "q_mm"], 1)
                    pe.wait_ge(S["halo_in"], s + 1)
                    pe.wait_ge(S["y"], s * TG)
                    for ft in range(KT):
                        for kt in range(KT):
                            ins = pe.matmul(PS[:, 4, ft * WIN:(ft + 1) * WIN],
                                            W[:, A_K + kt * D + ft * P:A_K + kt * D + (ft + 1) * P],
                                            xnT[:, kt, 0:WIN], start=(kt == 0), stop=(kt == KT - 1))
                    ins.then_inc(S["kh_mm"], 1)
                    for i in range(2 * TG):
                        bank = V_BANKS[i % 4]
                        if i >= 4:
                            pe.wait_ge(S["v"], s * 2 * TG + i - 3)
                        elif bank == 2:
                            pe.wait_ge(S["q_act"], s + 1)
                        elif bank == 3:
                            pe.wait_ge(S["q_dve"], s + 1)
                        else:
                            pe.wait_ge(S["k"], s * KT + bank + 1)
                        at = (i // 2) * P + (WIN if i % 2 else 0)
                        for kt in range(KT):
                            ins = pe.matmul(PS[:, bank, 0:D], xnT[:, kt, at:at + P],
                                            W[:, A_V + kt * D:A_V + (kt + 1) * D], start=(kt == 0), stop=(kt == KT - 1))
                        ins.then_inc(S["v_mm"], 1)
                    pe.wait_ge(S["v"], (s + 1) * 2 * TG)
                    pe.wait_ge(S["kh"], s + 1)

                    def scores(u):
                        j, g = u // HG, u % HG
                        pe.wait_ge(S["shift"], s * U + u - 1 if u >= 2 else s * U)
                        bank = PS[:, u % 2]
                        m = mask[:, c] if j == 0 else mask[:, 1]
                        pe.matmul(bank.rearrange("p (h t) -> p h t", h=4), identb[:],
                                  m.rearrange("p (o t) -> p o t", o=1).to_broadcast([P, 4, P]), start=True, stop=False)
                        for r in range(4):
                            for blk in range(2):
                                ins = pe.matmul(PS[WIN * blk:WIN * (blk + 1), u % 2, r * P:(r + 1) * P],
                                                qS[:, 4 * g + r, j * P + WIN * blk:j * P + WIN * (blk + 1)],
                                                kS[:, 4 * g // FH, j * P + WIN * blk:j * P + WIN * blk + P],
                                                start=False, stop=(r == 3))
                        ins.then_inc(S["s_mm"], 1)

                    def transp(u):
                        pe.wait_ge(S["exp"], s * U + u + 1)
                        pe.wait_ge(S["pT"], s * U + u - 1 if u >= 2 else s * U)
                        for r in range(4):
                            ins = pe.transpose(PS[:, 2 + u % 2, r * P:(r + 1) * P], pr[:, u % 3, r], ident[:])
                        ins.then_inc(S["p_tp"], 1)

                    def values(u):
                        j, g = u // HG, u % HG
                        pe.wait_ge(S["pT"], s * U + u + 1)
                        if g == 0:
                            pe.wait_ge(S["y"], s * TG + j - 1 if j >= 2 else s * TG)
                        for r in range(4):
                            h = 4 * g + r
                            for blk in range(2):
                                ins = pe.matmul(PS[WIN * blk:WIN * (blk + 1), 4 + j % 2, h * (HW + 1):(h + 1) * (HW + 1)],
                                                pT[:, u % 2, r, WIN * blk:WIN * (blk + 1)], V[:, blk, j, h],
                                                start=True, stop=True)
                        ins.then_inc(S["av"], 1)

                    def ytr(j):
                        n = s * TG + j + 1
                        pe.wait_ge(S["y"], n)
                        pe.wait_ge(S["yT"], n - 1)
                        for kt in range(KT):
                            ins = pe.transpose(PS[:, 6, kt * P:(kt + 1) * P], y[:, j % 2, kt * P:(kt + 1) * P], ident[:])
                        ins.then_inc(S["y_tp"], 1)

                    def project(j):
                        n = s * TG + j + 1
                        pe.wait_ge(S["yT"], n)
                        pe.wait_ge(S["o"], n - 1)
                        for kt in range(KT):
                            ins = pe.matmul(PS[:, 7, 0:D], yT[:, j % 2, kt], W[:, A_P + kt * D:A_P + (kt + 1) * D],
                                            start=(kt == 0), stop=(kt == KT - 1))
                        ins.then_inc(S["o_mm"], 1)

                    for u in range(U + 2):
                        if u < U:
                            scores(u)
                        if u >= 2:
                            values(u - 2)
                        if 1 <= u <= U:
                            transp(u - 1)
                        if u % HG == 3 and HG <= u < U:
                            ytr(u // HG - 1)
                        if u % HG == 0 and 2 * HG <= u < U:
                            project(u // HG - 2)
                    project(TG - 2)
                    features(s + 1)
                    ytr(TG - 1)
                    project(TG - 1)
                chunks(pe, body)
        signals.clear()


def hybrid(nc, x, norm_w, packs, packs2, dt_w, ident, unit_select, state_sum, bc_select, slot_pack, slot_rows, attn_pack,
           attn_mask, ident_bf16, out):
    scratch = lambda n: nc.dram_tensor(n, [TOK, D], F32, kind="Internal").ap()
    r, x1, x2, x3 = (scratch(n) for n in ("mamba_residual", "after_mamba", "after_slots", "after_attention"))
    first_norm(nc, x, r)
    mamba(nc, r, packs, packs2, dt_w, (ident, unit_select, state_sum, bc_select))
    second_norm(nc, x, r, x1, norm_w)
    slots(nc, "f1_", x1, x2, slot_pack, slot_rows, ident)
    attention(nc, x2, x3, attn_pack, attn_mask, ident, ident_bf16)
    slots(nc, "f2_", x3, out, slot_pack, slot_rows, ident)



def mamba_layout(np, a):
    f = lambda n: np.asarray(a["L0_attn_a_" + n])
    per = lambda v, n: v.reshape(n, P).T
    packs, packs2 = [], []
    for l in range(LAYERS):
        first = [f("in_proj_w")[l].T.reshape(KT, P, 2 * DI).transpose(1, 0, 2).reshape(P, -1),
                 f("conv_w")[l].reshape(CT, P, DC).transpose(1, 0, 2).reshape(P, -1),
                 per(f("conv_b")[l], CT), per(f("dt_proj_b")[l], CT), per(f("ln_w")[l], KT), per(f("ln_b")[l], KT)]
        second = [f("out_proj_w")[l].T.reshape(CT, P, D).transpose(1, 0, 2).reshape(P, -1),
                  np.pad(f("x_proj_w")[l].T.reshape(CT, P, R + 2 * NS).transpose(1, 0, 2),
                         ((0, 0), (0, 0), (0, XW - R - 2 * NS))).reshape(P, -1),
                  f("A_log")[l].reshape(CT, QU, JU, EU, NS).transpose(3, 4, 0, 2, 1).reshape(P, UNITS),
                  per(f("D_skip")[l], CT)]
        packs.append(np.concatenate(first, 1))
        packs2.append(np.concatenate(second, 1))
    m = np.arange(P)
    unit_select = np.zeros((PARTS * GC, JU, P), np.float32)
    state_sum = np.zeros((P, JU, GC), np.float32)
    for j in range(JU):
        for p in range(PARTS):
            unit_select[PARTS * (EU * j + m // NS) + p, j, m] = 1
        state_sum[m, j, EU * j + m // NS] = 1
    bc_select = np.zeros((P, 2, P), np.float32)
    dt_w = np.zeros((LAYERS, P, DI), f("dt_proj_w").dtype)
    for at in (0, XW):
        dt_w[:, at:at + R] = f("dt_proj_w").transpose(0, 2, 1)
        for i in range(2):
            bc_select[at + R + NS * i + m % NS, i, m] = 1
    return np.stack(packs), np.stack(packs2), dt_w, unit_select, state_sum, bc_select


def by_rows(w):
    return w.reshape(-1, P, w.shape[1]).transpose(1, 0, 2).reshape(P, -1)


def slot_layout(np, a):
    f = lambda n: np.asarray(a["L0_ffn_" + n])
    pack = np.concatenate([by_rows(f("w1").T), f("w2").T, by_rows(f("gru_wih").T), by_rows(f("gru_whh").T),
                           by_rows(f("wv").T), by_rows(f("wo").T), f("b1").reshape(P, 1), f("bv").reshape(KT, P).T,
                           np.tile(f("slot_init"), (2, 1)), np.tile(f("slot_scale"), (2, 1)),
                           np.broadcast_to(f("tau"), (P, 1))], 1)
    return pack, np.concatenate([f("b2"), f("gru_bih"), f("gru_bhh"), f("bo")])[None]


def attention_layout(np, a):
    f = lambda n: np.asarray(a["L0_attn_b_" + n])
    w, b = f("W_qkv"), f("b_qkv")
    heads = (np.arange(P)[:, None] // HW == np.arange(FH)[None]).astype(np.float32)
    pack = np.concatenate([by_rows(w[:, :D]), by_rows(w[:, D:2 * D]), by_rows(w[:, 2 * D:]), by_rows(f("W_proj")),
                           b[:D].reshape(KT, P).T, b[D:2 * D].reshape(KT, P).T, heads,
                           np.broadcast_to(b[2 * D:], (P, D)), np.broadcast_to(f("b_proj"), (P, D))], 1)
    q, k = np.arange(P)[:, None] % WIN, np.arange(P)[None]
    inner = np.where((k > q) & (k <= q + WIN), 0.0, NEG)
    first = inner.copy()
    first[:WIN, :WIN] = NEG
    return pack, np.stack([first, inner, inner, inner], 1)


def kernel(**inputs):
    import ml_dtypes
    import numpy as np
    import concourse.bacc as bacc
    from concourse.bass_utils import run_bass_kernel_spmd

    nc = bacc.Bacc("TRN2", target_bir_lowering=False, num_devices=1)
    bf16 = ml_dtypes.bfloat16
    x = np.asarray(inputs["L0_attn_a_x"])
    packs, packs2, dt_w, unit_select, state_sum, bc_select = mamba_layout(np, inputs)
    slot_pack, slot_rows = slot_layout(np, inputs)
    attn_pack, attn_mask = attention_layout(np, inputs)
    ident = np.eye(P, dtype=np.float32)
    norm_w = np.stack([np.broadcast_to(np.asarray(inputs["L0_attn_a_norm_f_" + n]), (P, D)) for n in "wb"], 1)
    given = dict(x=x.reshape(TOK, D), norm_w=norm_w, packs=packs, packs2=packs2, dt_w=dt_w, ident=ident,
                 unit_select=unit_select.astype(bf16), state_sum=state_sum, bc_select=bc_select, slot_pack=slot_pack,
                 slot_rows=slot_rows, attn_pack=attn_pack, attn_mask=attn_mask.astype(bf16), ident_bf16=ident.astype(bf16))
    arrays, args = {}, []
    for name, a in given.items():
        a = np.ascontiguousarray(a)
        arrays[f"in_{name}_dram"] = a
        args.append(nc.dram_tensor(f"in_{name}_dram", a.shape, mybir.dt.from_np(a.dtype), kind="ExternalInput").ap())
    args.append(nc.dram_tensor("out_dram", [TOK, D], F32, kind="ExternalOutput").ap())
    hybrid(nc, *args)
    got = run_bass_kernel_spmd(nc, [arrays], core_ids=[0])
    return got.results[0]["out_dram"].reshape(x.shape)
```
